# Optimizing a Trainium2 kernel written in Bass

```python
import numpy as np
import jax
import jax.numpy as jnp

def _softmax(x, axis=-1):
    return jax.nn.softmax(x, axis=axis)

def _gelu(x):
    return jax.nn.gelu(x, approximate=True)

def _silu(x):
    return jax.nn.silu(x)

def _sigmoid(x):
    return jax.nn.sigmoid(x)

def _layernorm(x, axis=-1, eps=1e-05):
    m = jnp.mean(x, axis=axis, keepdims=True)
    v = jnp.var(x, axis=axis, keepdims=True)
    return (x - m) / jnp.sqrt(v + eps)

def _scatter_add(tgt, idx, src, axis=0):
    return tgt.at[idx].add(src)

def _segment_sum(src, seg, n):
    return jax.ops.segment_sum(src, seg, n)
kernel_name = 'mk_prb_d1_jaxref_r4_4ffff2'

def setup_inputs(seed: int=0):
    np.random.seed(seed)
    _w = jnp.asarray

    def _L0_attn_setup():
        import jax, jax.numpy as jnp
        import numpy as np
        B_SZ, T, D_MODEL, N_STATE = (4, 1024, 256, 64)
        D_FF = (int(8 / 3 * D_MODEL) + 7) // 8 * 8
        EPS = 1e-06

        def _rmsnorm(x, w):
            rms = jnp.sqrt(jnp.mean(x * x, axis=-1, keepdims=True) + EPS)
            return x / rms * w
        key = jax.random.key(seed)
        ks = jax.random.split(key, 8)
        return {'x': jax.random.normal(ks[0], (B_SZ, T, D_MODEL), dtype=jnp.float32), 'log_lambda': jax.random.normal(ks[1], (N_STATE,), dtype=jnp.float32) * 0.5 + 3.0, 'B_w': jax.random.normal(ks[2], (N_STATE, D_MODEL), dtype=jnp.float32) / np.sqrt(D_MODEL), 'C_w': jax.random.normal(ks[3], (D_MODEL, N_STATE), dtype=jnp.float32) / np.sqrt(N_STATE), 'D_skip': jnp.zeros((D_MODEL,), dtype=jnp.float32), 'ssm_norm_w': jnp.ones((D_MODEL,), dtype=jnp.float32), 'ffn_norm_w': jnp.ones((D_MODEL,), dtype=jnp.float32), 'w1': jax.random.normal(ks[4], (D_FF, D_MODEL), dtype=jnp.float32) / np.sqrt(D_MODEL), 'w2': jax.random.normal(ks[5], (D_MODEL, D_FF), dtype=jnp.float32) / np.sqrt(D_FF), 'w3': jax.random.normal(ks[6], (D_FF, D_MODEL), dtype=jnp.float32) / np.sqrt(D_MODEL)}
    _L0_attn_in = _L0_attn_setup()

    def _L0_ffn_setup():
        import jax, jax.numpy as jnp
        import numpy as np
        E = 32
        H = 256
        I = 128
        G = 8
        TKG = 4
        TOPK = 8
        NSH = 2
        SCALE = 2.5
        key = jax.random.key(seed)
        ks = jax.random.split(key, 10)
        s = 0.02
        return {'hidden_states': jax.random.normal(ks[0], (2, 256, H), jnp.float32), 'gate_w': jax.random.normal(ks[1], (E, H), jnp.float32) * s, 'gate_bias': jax.random.normal(ks[2], (E,), jnp.float32) * s, 'w_gate': jax.random.normal(ks[3], (E, I, H), jnp.float32) * s, 'w_up': jax.random.normal(ks[4], (E, I, H), jnp.float32) * s, 'w_down': jax.random.normal(ks[5], (E, H, I), jnp.float32) * s, 'sh_gate': jax.random.normal(ks[6], (I * NSH, H), jnp.float32) * s, 'sh_up': jax.random.normal(ks[7], (I * NSH, H), jnp.float32) * s, 'sh_down': jax.random.normal(ks[8], (H, I * NSH), jnp.float32) * s}
    _L0_ffn_in = _L0_ffn_setup()
    _d = {'L0_attn_x': _L0_attn_in['x'], 'L0_attn_log_lambda': _L0_attn_in['log_lambda'], 'L0_attn_B_w': _L0_attn_in['B_w'], 'L0_attn_C_w': _L0_attn_in['C_w'], 'L0_attn_D_skip': _L0_attn_in['D_skip'], 'L0_attn_ssm_norm_w': _L0_attn_in['ssm_norm_w'], 'L0_attn_ffn_norm_w': _L0_attn_in['ffn_norm_w'], 'L0_attn_w1': _L0_attn_in['w1'], 'L0_attn_w2': _L0_attn_in['w2'], 'L0_attn_w3': _L0_attn_in['w3'], 'L0_ffn_gate_w': _L0_ffn_in['gate_w'], 'L0_ffn_gate_bias': _L0_ffn_in['gate_bias'], 'L0_ffn_w_gate': _L0_ffn_in['w_gate'], 'L0_ffn_w_up': _L0_ffn_in['w_up'], 'L0_ffn_w_down': _L0_ffn_in['w_down'], 'L0_ffn_sh_gate': _L0_ffn_in['sh_gate'], 'L0_ffn_sh_up': _L0_ffn_in['sh_up'], 'L0_ffn_sh_down': _L0_ffn_in['sh_down']}
    _x0 = _d['L0_attn_x']
    _d['L0_attn_x'] = jax.random.normal(jax.random.fold_in(jax.random.key(seed), 1), (16, 512, 256), dtype=_x0.dtype)
    del _x0
    return _d

def reference(L0_attn_x, L0_attn_log_lambda, L0_attn_B_w, L0_attn_C_w, L0_attn_D_skip, L0_attn_ssm_norm_w, L0_attn_ffn_norm_w, L0_attn_w1, L0_attn_w2, L0_attn_w3, L0_ffn_gate_w, L0_ffn_gate_bias, L0_ffn_w_gate, L0_ffn_w_up, L0_ffn_w_down, L0_ffn_sh_gate, L0_ffn_sh_up, L0_ffn_sh_down):

    def _L0_attn_ref(x, log_lambda, B_w, C_w, D_skip, ssm_norm_w, ffn_norm_w, w1, w2, w3):
        import jax, jax.numpy as jnp
        import numpy as np
        B_SZ, T, D_MODEL, N_STATE = (4, 1024, 256, 64)
        D_FF = (int(8 / 3 * D_MODEL) + 7) // 8 * 8
        EPS = 1e-06

        def _rmsnorm(x, w):
            rms = jnp.sqrt(jnp.mean(x * x, axis=-1, keepdims=True) + EPS)
            return x / rms * w
        u = _rmsnorm(x, ssm_norm_w)
        lam = jax.nn.sigmoid(log_lambda)
        Bu = jnp.einsum('btd,nd->btn', u, B_w)

        def step(h, bu_t):
            h = lam * h + bu_t
            return (h, h)
        h0 = jnp.zeros((x.shape[0], log_lambda.shape[0]), dtype=x.dtype)
        _, hs = jax.lax.scan(step, h0, jnp.swapaxes(Bu, 0, 1))
        hs = jnp.swapaxes(hs, 0, 1)
        y = jnp.einsum('btn,dn->btd', hs, C_w) + D_skip * u
        x = x + y
        z = _rmsnorm(x, ffn_norm_w)
        gate = jax.nn.silu(jnp.einsum('btd,fd->btf', z, w1))
        val = jnp.einsum('btd,fd->btf', z, w3)
        ffn = jnp.einsum('btf,df->btd', gate * val, w2)
        return x + ffn

    def _L0_ffn_ref(hidden_states, gate_w, gate_bias, w_gate, w_up, w_down, sh_gate, sh_up, sh_down):
        import jax, jax.numpy as jnp
        import numpy as np
        E = 32
        H = 256
        I = 128
        G = 8
        TKG = 4
        TOPK = 8
        NSH = 2
        SCALE = 2.5
        B, S, Hd = hidden_states.shape
        h = hidden_states.reshape(-1, Hd)
        logits = h.astype(jnp.float32) @ gate_w.T
        scores = jax.nn.sigmoid(logits)
        sc = scores + gate_bias
        grp = sc.reshape(-1, G, E // G)
        group_scores = jax.lax.top_k(grp, 2)[0].sum(-1)
        gidx = jax.lax.top_k(group_scores, TKG)[1]
        gmask = jnp.sum(jax.nn.one_hot(gidx, G, dtype=sc.dtype), axis=1)
        smask = jnp.repeat(gmask, E // G, axis=1)
        masked = jnp.where(smask > 0, sc, jnp.zeros_like(sc))
        tki = jax.lax.top_k(masked, TOPK)[1]
        tkw = jnp.take_along_axis(scores, tki, axis=1)
        tkw = tkw / (tkw.sum(-1, keepdims=True) + 1e-20)
        tkw = tkw * SCALE
        combine = (jax.nn.one_hot(tki, E, dtype=tkw.dtype) * tkw[..., None]).sum(1)
        g = jax.nn.silu(jnp.einsum('th,eih->tei', h, w_gate))
        u = jnp.einsum('th,eih->tei', h, w_up)
        routed = jnp.einsum('tei,ehi->th', g * u * combine[:, :, None], w_down)
        sg = jax.nn.silu(h @ sh_gate.T)
        shared = sg * (h @ sh_up.T) @ sh_down.T
        return (routed + shared).reshape(B, S, Hd)
    x = L0_attn_x
    xn = _layernorm(x, axis=-1)
    x = x + _L0_attn_ref(xn, L0_attn_log_lambda, L0_attn_B_w, L0_attn_C_w, L0_attn_D_skip, L0_attn_ssm_norm_w, L0_attn_ffn_norm_w, L0_attn_w1, L0_attn_w2, L0_attn_w3) + _L0_ffn_ref(xn, L0_ffn_gate_w, L0_ffn_gate_bias, L0_ffn_w_gate, L0_ffn_w_up, L0_ffn_w_down, L0_ffn_sh_gate, L0_ffn_sh_up, L0_ffn_sh_down)
    return x

_drawn_inputs = setup_inputs


def setup_inputs(seed=0):
    import zlib

    import numpy as np

    out = dict(_drawn_inputs(seed))
    spreads = {'L0_attn_D_skip': (0.0, 0.8),
     'L0_attn_ssm_norm_w': (1.0, 0.2),
     'L0_attn_ffn_norm_w': (1.0, 0.6)}
    factors = {'L0_ffn_gate_w': 8.0,
     'L0_ffn_gate_bias': 8.0,
     'L0_ffn_w_gate': 8.0,
     'L0_ffn_w_up': 8.0,
     'L0_ffn_w_down': 8.0,
     'L0_ffn_sh_gate': 8.0,
     'L0_ffn_sh_up': 8.0,
     'L0_ffn_sh_down': 8.0}
    for name, (base, spread) in spreads.items():
        noise = np.random.default_rng([zlib.crc32(name.encode()), seed]).standard_normal(out[name].shape)
        drawn = base * np.exp(spread * noise) if base else spread * noise
        out[name] = jnp.asarray(drawn.astype(out[name].dtype))
    for name, factor in factors.items():
        out[name] = (out[name] * factor).astype(out[name].dtype)
    return out
```

```python
from contextlib import ExitStack

import concourse.bass as bass
from concourse import mybir

P = 128
F32 = mybir.dt.float32
BF16 = mybir.dt.bfloat16
U32 = mybir.dt.uint32
ALU = mybir.AluOpType
ACT = mybir.ActivationFunctionType
AX_X = mybir.AxisListType.X
ds = bass.ds

D = 256
DC = D // P
N_STATE = 64
D_FF = 688
FT = -(-D_FF // P)
E = 32
NG = 8
EG = E // NG
TOP_GROUPS = 4
K = 8
INNER = 128
SHARED = 256
ROUTE_SCALE = 2.5
LN_EPS = 1e-5
RMS_EPS = 1e-6
ROW = D + 2
WEXP = 3 * D
GT = 4
G = GT * P


def is_(i, n):
    return isinstance(i, int) and i == n


class Steps:

    def __init__(self, eng, sem):
        self.eng, self.sem, self.base, self.n = eng, sem, 0, 0

    def done(self, ins):
        ins.then_inc(self.sem, 1)
        self.n += 1

    def wait(self):
        self.eng.wait_ge(self.sem, self.base + self.n)

    def enter(self, i, per):
        self.start = (self.base, self.n, per)
        self.base, self.n = self.base + self.n + i * per, 0

    def leave(self, count):
        base, n, per = self.start
        assert self.n == per, (self.n, per)
        self.base, self.n = base + n + count * per, 0


def build(nc, x, log_lambda, BT, CT, D_skip, ssm_w, ssm_w_col, ffn_w_col, w13T, w2T, gateT, gate_bias, wexp,
          shguT, shdT, out):
    T = x.shape[0]
    NT = T // P
    GROUPS = T // G
    NTILE = T * K // P + E
    NSLOT = NTILE * P
    PAIRS = NTILE // 2
    RING = 8
    CH = FT + SHARED // P
    NPAD = 2 * E
    TE_C = -(-NTILE // P)
    FAR = 1 << 20
    W = NT * E
    assert NPAD == NT and GROUPS == 16 and PAIRS % RING == 0 and NT % 4 == 0

    sorted_rows = nc.dram_tensor("sorted_rows", [NSLOT, ROW], F32).ap()
    expert_out = nc.dram_tensor("expert_out", [T * K, D], F32).ap()
    partial = nc.dram_tensor("partial", [T, D], F32).ap()
    tile_expert_dram = nc.dram_tensor("tile_expert_dram", [P * TE_C], U32).ap()

    with ExitStack() as ctx:
        def sb(name, shape, dt=F32):
            return ctx.enter_context(nc.sbuf_tensor(name, shape, dt))

        def sem(name):
            return ctx.enter_context(nc.semaphore(name))

        big = sb("big", [P, E * WEXP])
        xs = big[:, 0:NT * D].rearrange("p (t d) -> p t d", d=D)
        tables = big[:, NT * D:NT * D + 3 * W].rearrange("p (k n) -> p k n", k=3)
        order_te = tables[:, 0, :].rearrange("p (t e) -> p t e", e=E)
        weight_te = tables[:, 1, :].rearrange("p (t e) -> p t e", e=E)
        slot_te = tables[:, 2, :].rearrange("p (t e) -> p t e", e=E)

        w13 = sb("w13", [P, 2, DC, D_FF])
        w2 = sb("w2", [P, FT, D])
        shgu = sb("shgu", [P, 2, DC, SHARED])
        shd = sb("shd", [P, SHARED // P, D])
        bT = sb("bT", [P, DC, N_STATE])
        cT = sb("cT", [N_STATE, D])
        gT = sb("gT", [P, DC, E])
        skip_w = sb("skip_w", [P, D])
        ssmw_row = sb("ssmw_row", [P, D])
        ssmw_col = sb("ssmw_col", [P, DC])
        ffnw_col = sb("ffnw_col", [P, DC])
        bias_row = sb("bias_row", [P, E])
        loglam = sb("loglam", [N_STATE, 1])
        lam = sb("lam", [N_STATE, 1])
        ident = sb("ident", [P, P])
        before = sb("before", [P, P], BF16)
        ones_bf = sb("ones_bf", [P, P], BF16)
        codes = sb("codes", [P, NT * K], U32)
        order_c = sb("order_c", [P, K])
        ln_eps = sb("ln_eps", [P, 1])
        rms_eps = sb("rms_eps", [P, 1])
        stage = sb("stage", [P, K, ROW])
        stage_idx = sb("stage_idx", [P, K], U32)
        eq = sb("eq", [P, K // 2, E])
        eq_w = sb("eq_w", [P, K // 2, E])
        eq_s = sb("eq_s", [P, K // 2, E])
        pad_row = sb("pad_row", [P, ROW])
        pad_idx = sb("pad_idx", [P, 1], U32)
        pad_slots = sb("pad_slots", [P, NPAD], U32)
        bn6 = sb("bn6", [P, 2, GT, 6])
        mv4 = sb("mv4", [P, 2, GT, 2])
        mv = sb("mv", [P, NT, 2])
        rstd = sb("rstd", [P, NT])
        nmr = sb("nmr", [P, NT])
        rinv = sb("rinv", [P, NT])
        ssz = sb("ssz", [P, GT])
        rz = sb("rz", [P, GT])
        te_u = sb("te_u", [P, TE_C], U32)
        te_row = sb("te_row", [1, P * TE_C], U32)

        arena = sb("arena", [P, 13824])
        at = [0]

        def take(n):
            at[0] += n
            assert at[0] <= 13824
            return arena[:, at[0] - n:at[0]]

        a0_xn = [take(GT * D).rearrange("p (t d) -> p t d", d=D) for _ in range(2)]
        a0_xT = [take(DC * G).rearrange("p (c n) -> p c n", c=DC) for _ in range(2)]
        a0_sq = [take(GT * D).rearrange("p (t d) -> p t d", d=D) for _ in range(2)]
        at[0] = 0
        sc = take(W)
        masked = take(W)
        repl = take(W)
        sel = take(W)
        sel_et = take(W // 2).bitcast(BF16)
        small = take(9 * NT * NG).rearrange("p (k n) -> p k n", k=9)
        sc_te, masked_te, repl_te, sel_te = (
            a.rearrange("p (t e) -> p t e", e=E) for a in (sc, masked, repl, sel))
        logits, scores = tables[:, 0, :], tables[:, 1, :]
        reset = sc
        incl = masked
        incl_et = incl.rearrange("p (e t) -> p e t", e=E)
        ne = small[:, 0, 0:E]
        ntf = small[:, 1, 0:E]
        endt = small[:, 2, 0:E]
        base = small[:, 3, 0:E]
        nt_u = small[:, 4, 0:E].bitcast(U32)
        ones_e = small[:, 5, 0:E]
        end128 = small[:, 6, 0:E]
        pad_f = small[:, 7, 0:NPAD]
        pad_ge = small[:, 8, 0:E]
        den = small[:, 0, 64:64 + NT]
        rden = small[:, 1, 64:64 + NT]
        te_cmp = small[:, 2, 64:64 + TE_C * E].rearrange("p (c e) -> p c e", e=E)
        te_f = small[:, 3, 64:64 + TE_C]
        tail_i = sb("tail_i", [P, E], U32)
        tail_f = sb("tail_f", [P, E])
        tile_i = sb("tile_i", [P, TE_C], U32)
        tile_f = sb("tile_f", [P, TE_C])
        max8 = sb("max8", [P, NT, K])
        at[0] = 0
        xn = take(GT * D).rearrange("p (t d) -> p t d", d=D)
        xT = take(DC * G).rearrange("p (c n) -> p c n", c=DC)
        zT = take(DC * G).rearrange("p (c n) -> p c n", c=DC)
        bu = take(GT * N_STATE).rearrange("p (t n) -> p t n", n=N_STATE)
        hs = take(G)[0:N_STATE, :]
        lam_b = take(G)[0:N_STATE, :]
        x1 = take(GT * D).rearrange("p (t d) -> p t d", d=D)
        z = take(GT * D).rearrange("p (t d) -> p t d", d=D)
        part = [take(GT * D).rearrange("p (t d) -> p t d", d=D) for _ in range(2)]
        h = take(CH * G).rearrange("p (f n) -> p f n", n=G)
        gate = [take(G) for _ in range(2)]
        at[0] = 0
        rows = [take(2 * ROW).rearrange("p (s w) -> p s w", w=ROW) for _ in range(RING)]
        rT = [take(2 * D) for _ in range(2)]
        eg = [take(2 * INNER).rearrange("p (s i) -> p s i", i=INNER) for _ in range(2)]
        eh = [take(2 * INNER).rearrange("p (s i) -> p s i", i=INNER) for _ in range(2)]
        ehT = [take(2 * P) for _ in range(2)]
        ey = [take(2 * D).rearrange("p (s d) -> p s d", d=D) for _ in range(RING)]
        at[0] = 0
        f_y = [big[:, q * K * D:(q + 1) * K * D] for q in range(4)]
        f_part = [take(D) for _ in range(4)]
        f_out = [take(D) for _ in range(4)]
        f_sum = [take(K * D // 2) for _ in range(2)]

        ps = ctx.enter_context(nc.psum_tensor("ps", [P, 8, 512], F32))

        x_loaded = [sem(f"x_loaded{j}") for j in range(4)]
        consts_loaded = sem("consts_loaded")
        consts_made = sem("consts_made")
        pool_step = sem("pool_step")
        dve_step = sem("dve_step")
        act_step = sem("act_step")
        var_ready = sem("var_ready")
        std_ready = sem("std_ready")
        a0_xn_ready = sem("a0_xn_ready")
        a0_xn_free = sem("a0_xn_free")
        a0_xposed = sem("a0_xposed")
        a0_xT_ready = sem("a0_xT_ready")
        a0_logits_ready = sem("a0_logits_ready")
        a0_logits_used = sem("a0_logits_used")
        scores_ready = sem("scores_ready")
        rms_x_ready = sem("rms_x_ready")
        weights_folded = sem("weights_folded")
        sel_ready = sem("sel_ready")
        ranks_ready = sem("ranks_ready")
        routing_done = sem("routing_done")
        te_ready = sem("te_ready")
        te_stored = sem("te_stored")
        te_loaded = sem("te_loaded")
        lam_ready = sem("lam_ready")

        xn_ready = sem("xn_ready")
        xposed = sem("xposed")
        xT_ready = sem("xT_ready")
        bu_ready = sem("bu_ready")
        bu_scaled = sem("bu_scaled")
        buT_ready = sem("buT_ready")
        hs_ready = sem("hs_ready")
        y_ready = sem("y_ready")
        x1_ready = sem("x1_ready")
        rms_z_ready = sem("rms_z_ready")
        z_ready = sem("z_ready")
        zposed = sem("zposed")
        zT_ready = sem("zT_ready")
        gu_ready = sem("gu_ready")
        gate_ready = sem("gate_ready")
        h_made = sem("h_made")
        down_ready = sem("down_ready")
        part_ready = sem("part_ready")
        part_stored = [sem(f"part_stored{j}") for j in range(2)]
        stage_x = [sem(f"stage_x{j}") for j in range(2)]
        stage_meta = [sem(f"stage_meta{j}") for j in range(2)]
        scattered = [sem(f"scattered{j}") for j in range(2)]
        pad_scattered = sem("pad_scattered")
        wexp_loaded = sem("wexp_loaded")

        rows_loaded = [sem(f"rows_loaded{j}") for j in range(RING)]
        rposed = sem("rposed")
        rT_ready = sem("rT_ready")
        egu_ready = sem("egu_ready")
        eg_ready = sem("eg_ready")
        eh_ready = sem("eh_ready")
        ehposed = sem("ehposed")
        ehT_ready = sem("ehT_ready")
        ey_ready = sem("ey_ready")
        ey_act = sem("ey_act")
        ey_dve = sem("ey_dve")
        ey_stored = [sem(f"ey_stored{j}") for j in range(RING)]
        f_loaded = [sem(f"f_loaded{j}") for j in range(4)]
        f_summed = [sem(f"f_summed{j}") for j in range(4)]
        f_stored = [sem(f"f_stored{j}") for j in range(4)]

        block = ctx.enter_context(nc.Block())

        CONSTS = 14

        def f_rows(s):
            return P if s < CH - 1 else D_FF - (FT - 1) * P

        def apart(eng, *waits):
            values = [v if isinstance(v, int) else eng.to_reg(v) for _, v in waits]
            eng.wait_ge(consts_made, 1)
            for (s, _), v in zip(waits, values):
                eng.wait_ge(s, v)

        def groups(eng, body, step=None, per=0):
            body(0, 0)
            with eng.Fori(0, GROUPS // 2 - 1) as it:
                if step:
                    step.enter(it, per)
                for j in range(2):
                    body(2 * it + 1 + j, 1 - j)
                if step:
                    step.leave(GROUPS // 2 - 1)
            body(GROUPS - 1, 1)

        def first_apart(eng, count, body):
            body(0)
            with eng.Fori(1, count) as i:
                body(i)

        def pairs(eng, body):
            for n in range(1, RING):
                body(n, n)
            with eng.Fori(0, PAIRS // RING - 2) as it:
                for q in range(RING):
                    body(RING * it + RING + q, q)
            for q in range(RING):
                body(PAIRS - RING + q, q)

        @block.sync
        def _(sp):
            def load_x(it):
                for j in range(4):
                    if not is_(it, 0):
                        sp.wait_ge(x_loaded[j], 16 * it)
                    sp.dma_start(xs[:, ds((4 * it + j) * GT, GT), :],
                                 x[ds((4 * it + j) * G, G), :].rearrange("(t p) d -> p t d", p=P)
                                 ).then_inc(x_loaded[j], 16)

            first_apart(sp, GROUPS // 4, load_x)
            sp.wait_ge(te_ready, 1)
            sp.dma_start(tile_expert_dram.rearrange("(p c) -> p c", c=TE_C), te_u[:, :]).then_inc(te_stored, 16)
            sp.wait_ge(te_stored, 16)
            sp.dma_start(te_row[:, :], tile_expert_dram.rearrange("(a n) -> a n", a=1)).then_inc(te_loaded, 16)

            def store_part(g, par):
                sp.wait_ge(part_ready, g + 1)
                sp.dma_start(partial[ds(g * G, G), :].rearrange("(t p) d -> p t d", p=P), part[par]
                             ).then_inc(part_stored[par], 16)
                sp.wait_ge(stage_x[1], GT * (g + 1))
                sp.dma_start(big[:, ds(g * GT * D, GT * D)], wexp[:, ds(g * GT * D, GT * D)]
                             ).then_inc(wexp_loaded, 16)

            with sp.Fori(0, GROUPS // 2) as it:
                for par in range(2):
                    store_part(2 * it + par, par)
            sp.dma_start(big[:, NT * D:], wexp[:, NT * D:]).then_inc(wexp_loaded, 16)
            sp.wait_ge(scattered[0], 16 * (K // 2) * NT)
            sp.wait_ge(scattered[1], 16 * (K // 2) * NT)
            sp.wait_ge(pad_scattered, 16 * NPAD)
            sp.wait_ge(part_stored[0], 16 * GROUPS // 2)
            sp.wait_ge(part_stored[1], 16 * GROUPS // 2)

            def load_rows(it):
                for q in range(RING):
                    if not is_(it, 0):
                        sp.wait_ge(ey_stored[q], 32 * it)
                    sp.dma_start(rows[q], sorted_rows[ds((RING * it + q) * 2 * P, 2 * P), :]
                                 .rearrange("(s p) w -> p s w", p=P)).then_inc(rows_loaded[q], 16)

            first_apart(sp, PAIRS // RING, load_rows)
            for q in range(RING):
                sp.wait_ge(ey_stored[q], 32 * (PAIRS // RING))

            def load_results(it):
                for q in range(4):
                    if not is_(it, 0):
                        sp.wait_ge(f_summed[q], it)
                    sp.dma_start(f_y[q], expert_out[ds((4 * it + q) * P * K, P * K), :]
                                 .rearrange("(p k) d -> p (k d)", k=K)).then_inc(f_loaded[q], 16)
                    sp.dma_start(f_part[q], partial[ds((4 * it + q) * P, P), :]).then_inc(f_loaded[q], 16)

            first_apart(sp, NT // 4, load_results)

        @block.gpsimd
        def _(pool):
            step = Steps(pool, pool_step)
            step.done(nc.gpsimd.memset(ident[:, :], 0.0))
            step.done(nc.gpsimd.memset(before[:, :], 1.0))
            nc.gpsimd.memset(ones_bf[:, :], 1.0)
            for k in range(K):
                nc.gpsimd.memset(order_c[:, k:k + 1], float(k - 100))
            nc.gpsimd.memset(ln_eps[:, :], LN_EPS)
            nc.gpsimd.memset(rms_eps[:, :], RMS_EPS)
            step.done(nc.gpsimd.memset(pad_row[:, :], 0.0))
            nc.gpsimd.iota(codes[:, :].rearrange("p (t k) -> p t k", k=K), pattern=[[P * K, NT], [1, K]], base=0,
                           channel_multiplier=K)
            nc.gpsimd.iota(tail_i[:, :], pattern=[[P, E]], base=0, channel_multiplier=1)
            nc.gpsimd.iota(tile_i[:, :], pattern=[[1, TE_C]], base=0, channel_multiplier=TE_C)
            step.wait()
            nc.gpsimd.affine_select(out=ident[:, :], in_=ident[:, :], compare_op=ALU.not_equal, fill=1.0, base=0,
                                    pattern=[[-1, P]], channel_multiplier=1)
            nc.gpsimd.affine_select(out=before[:, :], in_=before[:, :], compare_op=ALU.is_gt, fill=0.0, base=0,
                                    pattern=[[1, P]], channel_multiplier=-1)
            nc.gpsimd.iota(pad_row[:, D:D + 1].bitcast(U32), pattern=[[0, 1]], base=FAR, channel_multiplier=0
                           ).then_inc(consts_made, 1)
            pool.wait_ge(routing_done, 1)

            def scatter_tile(i):
                for half in range(2):
                    apart(pool, (stage_x[half], i + 1), (stage_meta[half], i + 1))
                    for k in range(K // 2 * half, K // 2 * (half + 1)):
                        pool.indirect_dma_start(
                            out=sorted_rows, out_offset=bass.IndirectOffsetOnAxis(ap=stage_idx[:, k:k + 1], axis=0),
                            in_=stage[:, k, :], in_offset=None).then_inc(scattered[half], 16)
                if not is_(i, 0):
                    apart(pool, (pad_scattered, 16 * i))
                nc.gpsimd.tensor_copy(pad_idx[:, :], pad_slots[:, ds(i, 1)]).then_inc(pool_step, 1)
                apart(pool, (pool_step, i + (step.n + 1)))
                pool.indirect_dma_start(
                    out=sorted_rows, out_offset=bass.IndirectOffsetOnAxis(ap=pad_idx[:, 0:1], axis=0),
                    in_=pad_row[:, :], in_offset=None, bounds_check=NSLOT - 1, oob_is_err=False
                ).then_inc(pad_scattered, 16)

            first_apart(pool, NT, scatter_tile)
            with pool.Fori(0, PAIRS // RING) as it:
                for q in range(RING):
                    apart(pool, (ey_act, RING * it + (q + 1)), (ey_dve, RING * it + (q + 1)))
                    for s in range(2):
                        pool.indirect_dma_start(
                            out=expert_out,
                            out_offset=bass.IndirectOffsetOnAxis(ap=rows[q].bitcast(U32)[:, s, D:D + 1], axis=0),
                            in_=ey[q][:, s, :], in_offset=None, bounds_check=T * K - 1, oob_is_err=False
                        ).then_inc(ey_stored[q], 16)

        @block.scalar
        def _(act):
            step = Steps(act, act_step)
            for dst, src in ((gT[:, :, :], gateT), (bias_row[:, :], gate_bias.partition_broadcast(P)),
                             (bT[:, :, :], BT), (cT[:, :], CT), (skip_w[:, :], D_skip.partition_broadcast(P)),
                             (ssmw_row[:, :], ssm_w.partition_broadcast(P)), (ssmw_col[:, :], ssm_w_col),
                             (ffnw_col[:, :], ffn_w_col), (loglam[:, :], log_lambda.rearrange("(n a) -> n a", a=1)),
                             (w13[:, :, :, :], w13T),
                             (w2[:, 0:FT - 1, :], w2T[0:(FT - 1) * P, :].rearrange("(f p) d -> p f d", p=P)),
                             (w2[0:D_FF - (FT - 1) * P, FT - 1, :], w2T[(FT - 1) * P:, :]),
                             (shgu[:, :, :, :], shguT), (shd[:, :, :], shdT)):
                act.dma_start(dst, src).then_inc(consts_loaded, 16)
            act.wait_ge(consts_made, 1)
            act.wait_ge(var_ready, 1)
            nc.scalar.activation(rstd[:, :], mv[:, :, 1], ACT.Sqrt, bias=ln_eps[:, :]).then_inc(std_ready, 1)

            def a0_copy(g, par):
                act.wait_ge(a0_xposed, g + 1)
                for c in range(DC):
                    last = nc.scalar.activation(a0_xT[par][:, c, :], ps[:, 2 * par + c, :], ACT.Copy)
                last.then_inc(a0_xT_ready, 1)
                for t in range(GT):
                    last = nc.scalar.activation(a0_sq[par][:, t, :], a0_xn[par][:, t, :], ACT.Square,
                                                accum_out=rinv[:, ds(g * GT + t, 1)])
                last.then_inc(a0_xn_free, 1)

            def a0_evacuate(g, par):
                act.wait_ge(a0_logits_ready, g + 1)
                nc.scalar.activation(logits[:, ds(g * GT * E, GT * E)], ps[:, 4 + par, 0:GT * E], ACT.Copy
                                     ).then_inc(act_step, 1)

            a0_copy(0, 0)
            with act.Fori(0, GROUPS // 2 - 1) as it:
                for par in range(2):
                    a0_copy(2 * it + par + 1, 1 - par)
                    a0_evacuate(2 * it + par, par)
            a0_copy(GROUPS - 1, 1)
            a0_evacuate(GROUPS - 2, 0)
            a0_evacuate(GROUPS - 1, 1)
            step.n += GROUPS
            step.wait()
            nc.scalar.activation(scores, logits, ACT.Sigmoid).then_inc(scores_ready, 1)
            act.wait_ge(consts_loaded, 16 * CONSTS)
            nc.scalar.activation(lam[:, :], loglam[:, :], ACT.Sigmoid).then_inc(lam_ready, 1)
            nc.scalar.activation(rinv[:, :], rinv[:, :], ACT.Sqrt, bias=rms_eps[:, :], scale=1.0 / D
                                 ).then_inc(rms_x_ready, 1)

            def xT_copy(n):
                act.wait_ge(xposed, n + 1)
                for c in range(DC):
                    last = nc.scalar.activation(xT[:, c, :], ps[:, c, :], ACT.Copy)
                last.then_inc(xT_ready, 1)

            def rms_z(n):
                act.wait_ge(x1_ready, n + 1)
                for t in range(GT):
                    last = nc.scalar.activation(z[:, t, :], x1[:, t, :], ACT.Square, accum_out=ssz[:, t:t + 1])
                step.done(last)
                step.wait()
                nc.scalar.activation(ssz[:, :], ssz[:, :], ACT.Sqrt, bias=rms_eps[:, :], scale=1.0 / D
                                     ).then_inc(rms_z_ready, 1)

            def zT_copy(n):
                act.wait_ge(zposed, n + 1)
                for c in range(DC):
                    last = nc.scalar.activation(zT[:, c, :], ps[:, c, :], ACT.Copy)
                last.then_inc(zT_ready, 1)

            def gate_tile(g, s):
                act.wait_ge(gu_ready, CH * g + s + 1)
                if not is_(g, 0) or s >= 2:
                    act.wait_ge(h_made, CH * g + s - 1)
                m = f_rows(s)
                nc.scalar.activation(gate[s % 2][0:m, :], ps[0:m, 2 + 2 * (s % 2), :], ACT.Silu
                                     ).then_inc(gate_ready, 1)

            def stage_half(i, half):
                if not is_(i, 0):
                    apart(act, (scattered[half], 16 * (K // 2) * i))
                nc.scalar.activation(stage[:, K // 2 * half:K // 2 * (half + 1), 0:D],
                                     xs[:, ds(i, 1), :].to_broadcast([P, K // 2, D]), ACT.Identity,
                                     bias=nmr[:, ds(i, 1)], scale=rstd[:, ds(i, 1)]).then_inc(stage_x[half], 1)

            def act_group(g, par):
                more = not is_(g, GROUPS - 1)
                for s in range(CH):
                    gate_tile(g, s)
                    stage_half(g * GT + s // 2, s % 2)
                    if more and s == 1:
                        xT_copy(g + 1)
                    if more and s == 5:
                        rms_z(g + 1)
                if more:
                    zT_copy(g + 1)

            act.wait_ge(routing_done, 1)
            xT_copy(0)
            rms_z(0)
            zT_copy(0)
            groups(act, act_group, step, 2)

            def rT_copy(n, par):
                act.wait_ge(rposed, n + 1)
                nc.scalar.activation(rT[par], ps[:, par, :], ACT.Copy).then_inc(rT_ready, 1)

            def e_gate(n, par):
                act.wait_ge(egu_ready, n + 1)
                nc.scalar.activation(
                    eg[par], ps[:, 2 + par, :].rearrange("p (s u i) -> p s u i", s=2, u=2)[:, :, 0, :], ACT.Silu
                ).then_inc(eg_ready, 1)

            def e_out(n, q):
                act.wait_ge(ey_ready, n + 1)
                nc.scalar.activation(ey[q][:, 0, :], ps[:, 6, 0:D], ACT.Copy, scale=rows[q][:, 0, D + 1:D + 2]
                                     ).then_inc(ey_act, 1)

            def act_pair(n, q):
                e_gate(n, q % 2)
                if not is_(n, PAIRS - 1):
                    rT_copy(n + 1, (q + 1) % 2)
                e_out(n - 1, (q + RING - 1) % RING)

            rT_copy(0, 0)
            e_gate(0, 0)
            rT_copy(1, 1)
            pairs(act, act_pair)
            e_out(PAIRS - 1, RING - 1)

            with act.Fori(0, NT // 4) as it:
                for q in range(4):
                    act.wait_ge(f_summed[q], it + 1)
                    act.dma_start(out[ds((4 * it + q) * P, P), :], f_out[q]).then_inc(f_stored[q], 16)
            for q in range(4):
                act.wait_ge(f_stored[q], 16 * (NT // 4))

        @block.vector
        def _(dve):
            step = Steps(dve, dve_step)
            tt, tsc = nc.vector.tensor_tensor, nc.vector.tensor_scalar

            def do(ins):
                step.done(ins)
                step.wait()

            with dve.Fori(0, GROUPS // 4) as it:
                step.enter(it, 12)
                for j in range(4):
                    dve.wait_ge(x_loaded[j], 16 * (it + 1))
                    for t in range(GT):
                        last = nc.vector.bn_stats(bn6[:, j % 2, t, :], xs[:, ds((4 * it + j) * GT + t, 1), :]
                                                  .rearrange("p t d -> p (t d)"))
                    step.done(last)
                    apart(dve, (dve_step, step.base + step.n))
                    for t in range(GT):
                        last = nc.vector.bn_aggr(mv4[:, j % 2, t, :], bn6[:, j % 2, t, :])
                    do(last)
                    step.done(nc.vector.tensor_copy(mv[:, ds((4 * it + j) * GT, GT), :], mv4[:, j % 2, :, :]))
                step.leave(GROUPS // 4)
            step.wait()
            dve.sem_inc(var_ready, 1)
            dve.wait_ge(std_ready, 1)
            do(nc.vector.reciprocal(rstd[:, :], rstd[:, :]))
            do(nc.vector.scalar_tensor_tensor(nmr[:, :], mv[:, :, 0], -1.0, rstd[:, :], ALU.mult, ALU.mult))

            def normalise(dst, g):
                for t in range(GT):
                    i = g * GT + t
                    last = tsc(dst[:, t, :], xs[:, ds(i, 1), :].rearrange("p t d -> p (t d)"),
                               rstd[:, ds(i, 1)], nmr[:, ds(i, 1)], ALU.mult, ALU.add)
                return last

            normalise(a0_xn[0], 0).then_inc(a0_xn_ready, 1)
            normalise(a0_xn[1], 1).then_inc(a0_xn_ready, 1)
            with dve.Fori(0, GROUPS // 2 - 1) as it:
                for par in range(2):
                    dve.wait_ge(a0_xn_free, 2 * it + par + 1)
                    normalise(a0_xn[par], 2 * it + par + 2).then_inc(a0_xn_ready, 1)

            dve.wait_ge(consts_loaded, 16 * CONSTS)
            for c in range(DC):
                tsc(bT[:, c, :], bT[:, c, :], ssmw_col[:, c:c + 1], None, ALU.mult)
                for m in range(2):
                    tsc(w13[:, m, c, :], w13[:, m, c, :], ffnw_col[:, c:c + 1], None, ALU.mult)
            tt(skip_w[:, :], skip_w[:, :], ssmw_row[:, :], ALU.mult).then_inc(weights_folded, 1)

            dve.wait_ge(scores_ready, 1)
            scores_te = scores.rearrange("p (t e) -> p t e", e=E)
            do(tt(sc_te, scores_te, bias_row[:, :].unsqueeze(1).to_broadcast([P, NT, E]), ALU.add))
            v = [sc.rearrange("p (n j) -> p n j", j=EG)[:, :, j] for j in range(EG)]
            hi01, lo01, hi23, lo23, gs = (small[:, k, :] for k in range(5))
            tt(hi01, v[0], v[1], ALU.max)
            tt(lo01, v[0], v[1], ALU.min)
            tt(hi23, v[2], v[3], ALU.max)
            do(tt(lo23, v[2], v[3], ALU.min))
            tt(gs, hi01, hi23, ALU.max)
            tt(hi01, hi01, hi23, ALU.min)
            do(tt(lo01, lo01, lo23, ALU.max))
            do(tt(hi01, hi01, lo01, ALU.max))
            do(tt(gs, gs, hi01, ALU.add))
            gs_tg = gs.rearrange("p (t g) -> p t g", g=NG)
            rank_tg = small[:, 5, :].rearrange("p (t g) -> p t g", g=NG)
            beats = small[:, 6, :].rearrange("p (t g) -> p t g", g=NG)
            for g in range(NG):
                last = nc.vector.memset(rank_tg[:, :, g:g + 1], float(NG - 1 - g))
            do(last)
            for s in range(1, NG):
                do(tt(beats[:, :, 0:NG - s], gs_tg[:, :, 0:NG - s], gs_tg[:, :, s:NG], ALU.is_ge))
                do(tt(rank_tg[:, :, s:NG], rank_tg[:, :, s:NG], beats[:, :, 0:NG - s], ALU.add))
                do(tt(rank_tg[:, :, 0:NG - s], rank_tg[:, :, 0:NG - s], beats[:, :, 0:NG - s], ALU.subtract))
            do(tsc(beats, rank_tg, float(TOP_GROUPS), None, ALU.is_lt))
            do(tt(masked.rearrange("p (n j) -> p n j", j=EG), sc.rearrange("p (n j) -> p n j", j=EG),
                  small[:, 6, :].unsqueeze(2).to_broadcast([P, NT * NG, EG]), ALU.mult))
            for t in range(NT):
                last = nc.vector.max(max8[:, t, :], masked_te[:, t, :])
            do(last)
            for t in range(NT):
                last = nc.vector.match_replace(repl_te[:, t, :], max8[:, t, :], masked_te[:, t, :], -1e30)
            do(last)
            tt(sel_et.rearrange("p (e t) -> p t e", t=NT), repl_te, masked_te, ALU.not_equal).then_inc(sel_ready, 1)
            do(tt(sel, repl, masked, ALU.not_equal))
            do(nc.vector.memset(reset, 1.0))
            do(nc.vector.memset(reset.rearrange("p (t e) -> p t e", e=E)[:, :, 0:1], 0.0))
            do(nc.vector.tensor_tensor_scan(incl, reset, sel, 0.0, ALU.mult, ALU.add))
            do(nc.vector.scalar_tensor_tensor(order_te, sel_te, -101.0, incl.rearrange("p (t e) -> p t e", e=E),
                                              ALU.mult, ALU.add))
            do(tt(weight_te, scores_te, sel_te, ALU.mult))
            do(nc.vector.tensor_reduce(den, weight_te, AX_X, ALU.add))
            do(tsc(den, den, 1e-20, None, ALU.add))
            do(nc.vector.reciprocal(rden, den))
            do(tsc(rden, rden, ROUTE_SCALE, None, ALU.mult))
            do(tt(weight_te, weight_te, rden.unsqueeze(2).to_broadcast([P, NT, E]), ALU.mult))
            do(nc.vector.memset(reset, 1.0))
            do(nc.vector.memset(reset.rearrange("p (e t) -> p e t", t=NT)[:, :, 0:1], 0.0))
            dve.wait_ge(ranks_ready, 1)
            for b in range(4):
                r = slice(512 * b, 512 * (b + 1))
                last = nc.vector.tensor_tensor_scan(incl[:, r], reset[:, r], ps[:, b, :], 0.0, ALU.mult, ALU.add)
            do(last)
            nc.vector.tensor_copy(ne, incl_et[:, :, NT - 1])
            for b in range(4):
                r = slice(512 * b, 512 * (b + 1))
                last = tt(repl[:, r], incl[:, r], ps[:, b, :], ALU.subtract)
            do(last)
            for b in range(4):
                r = slice(512 * b, 512 * (b + 1))
                last = tt(repl[:, r], repl[:, r], ps[:, 4 + b, :], ALU.add)
            do(last)
            do(tsc(nt_u, ne, float(P - 1), None, ALU.add))
            do(tsc(nt_u, nt_u, 7, None, ALU.logical_shift_right))
            nc.vector.memset(ones_e, 1.0)
            do(nc.vector.tensor_copy(ntf, nt_u))
            do(nc.vector.tensor_tensor_scan(endt, ones_e, ntf, 0.0, ALU.mult, ALU.add))
            do(tt(base, endt, ntf, ALU.subtract))
            do(tsc(base, base, float(P), None, ALU.mult))
            do(tt(slot_te.rearrange("p t e -> p e t"), repl.rearrange("p (e t) -> p e t", t=NT),
                  base.unsqueeze(2).to_broadcast([P, E, NT]), ALU.add))
            dve.wait_ge(consts_made, 1)
            nc.vector.tensor_copy(tail_f[:, :], tail_i[:, :])
            nc.vector.tensor_copy(tile_f[:, :], tile_i[:, :])
            tsc(end128, endt, float(P), None, ALU.mult)
            do(tt(pad_f[:, 0:E], base, ne, ALU.add))
            do(tsc(pad_f[:, 0:E], pad_f[:, 0:E], tail_f[:, 0:1], None, ALU.add))
            do(tt(pad_ge, pad_f[:, 0:E], end128, ALU.is_ge))
            do(nc.vector.scalar_tensor_tensor(pad_f[:, 0:E], pad_ge, float(FAR), pad_f[:, 0:E], ALU.mult, ALU.add))
            do(tsc(pad_f[:, E:], tail_f[:, :], end128[:, E - 1:E], None, ALU.add))
            nc.vector.tensor_copy(pad_slots[:, :], pad_f)
            do(tt(te_cmp, tile_f[:, :].unsqueeze(2).to_broadcast([P, TE_C, E]),
                  endt.unsqueeze(1).to_broadcast([P, TE_C, E]), ALU.is_ge))
            do(nc.vector.tensor_reduce(te_f, te_cmp, AX_X, ALU.add))
            do(tsc(te_f, te_f, float(E - 1), float(WEXP), ALU.min, ALU.mult))
            nc.vector.tensor_copy(te_u[:, :], te_f).then_inc(te_ready, 1)
            dve.wait_ge(lam_ready, 1)
            do(nc.vector.memset(lam_b, 1.0))
            tsc(lam_b, lam_b, lam[:, :], None, ALU.mult)
            dve.wait_ge(rms_x_ready, 1)
            do(nc.vector.reciprocal(rinv[:, :], rinv[:, :]))
            dve.sem_inc(routing_done, 1)

            def a1_norm(n):
                normalise(xn, n).then_inc(xn_ready, 1)

            def bu_scale(n):
                dve.wait_ge(bu_ready, n + 1)
                tt(bu, ps[:, 0, 0:GT * N_STATE].rearrange("p (t n) -> p t n", n=N_STATE),
                   rinv[:, ds(n * GT, GT)].unsqueeze(2).to_broadcast([P, GT, N_STATE]), ALU.mult
                   ).then_inc(bu_scaled, 1)

            def scan(n):
                dve.wait_ge(buT_ready, n + 1)
                nc.vector.tensor_tensor_scan(hs, lam_b, ps[0:N_STATE, 1, :], 0.0, ALU.mult, ALU.add
                                             ).then_inc(hs_ready, 1)

            def make_x1(n, par):
                for t in range(GT):
                    last = nc.vector.scalar_tensor_tensor(z[:, t, :], xn[:, t, :], rinv[:, ds(n * GT + t, 1)],
                                                          skip_w[:, :], ALU.mult, ALU.mult)
                do(last)
                do(tt(z, z, xn, ALU.add))
                dve.wait_ge(y_ready, n + 1)
                for b in range(2):
                    last = tt(x1[:, 2 * b:2 * b + 2, :], z[:, 2 * b:2 * b + 2, :],
                              ps[:, b, :].rearrange("p (t d) -> p t d", d=D), ALU.add)
                last.then_inc(x1_ready, 1)
                dve.wait_ge(x1_ready, n + 1)
                dve.wait_ge(part_stored[par], 8 * (n - par))
                tt(part[par], xs[:, ds(n * GT, GT), :], x1, ALU.add)

            def make_z(n):
                dve.wait_ge(rms_z_ready, n + 1)
                do(nc.vector.reciprocal(rz[:, :], ssz[:, :]))
                for t in range(GT):
                    last = tsc(z[:, t, :], x1[:, t, :], rz[:, t:t + 1], None, ALU.mult)
                last.then_inc(z_ready, 1)

            def h_tile(g, s):
                m = f_rows(s)
                dve.wait_ge(gate_ready, CH * g + s + 1)
                tt(h[0:m, s, :], gate[s % 2][0:m, :], ps[0:m, 3 + 2 * (s % 2), :], ALU.mult).then_inc(h_made, 1)

            def stage_meta_half(i, half):
                ks = slice(K // 2 * half, K // 2 * (half + 1))
                shape = [P, K // 2, E]
                if not is_(i, 0):
                    dve.wait_ge(scattered[half], 16 * (K // 2) * i)
                do(tt(eq[:, :, :], order_te[:, ds(i, 1), :].to_broadcast(shape),
                      order_c[:, ks].unsqueeze(2).to_broadcast(shape), ALU.is_equal))
                tt(eq_w[:, :, :], eq[:, :, :], weight_te[:, ds(i, 1), :].to_broadcast(shape), ALU.mult)
                do(tt(eq_s[:, :, :], eq[:, :, :], slot_te[:, ds(i, 1), :].to_broadcast(shape), ALU.mult))
                nc.vector.tensor_reduce(stage[:, ks, D + 1], eq_w[:, :, :], AX_X, ALU.add)
                nc.vector.tensor_copy(stage[:, ks, D].bitcast(U32), codes[:, ds(i * K + K // 2 * half, K // 2)])
                with nc.allow_low_precision(reason="one term of each sum isn't zero, an integer below 2**24"):
                    nc.vector.tensor_reduce(stage_idx[:, ks], eq_s[:, :, :], AX_X, ALU.add
                                            ).then_inc(stage_meta[half], 1)

            def finish_part(g, par):
                dve.wait_ge(down_ready, g + 1)
                for b in range(2):
                    last = tt(part[par][:, 2 * b:2 * b + 2, :], part[par][:, 2 * b:2 * b + 2, :],
                              ps[:, 6 + b, :].rearrange("p (t d) -> p t d", d=D), ALU.add)
                last.then_inc(part_ready, 1)

            def dve_group(g, par):
                more = not is_(g, GROUPS - 1)
                if more:
                    a1_norm(g + 1)
                for s in range(CH):
                    h_tile(g, s)
                    if more and s == 6:
                        make_z(g + 1)
                    stage_meta_half(g * GT + s // 2, s % 2)
                    if more and s == 2:
                        bu_scale(g + 1)
                    if more and s == 3:
                        scan(g + 1)
                    if more and s == 4:
                        make_x1(g + 1, 1 - par)
                finish_part(g, par)

            a1_norm(0)
            bu_scale(0)
            scan(0)
            make_x1(0, 0)
            make_z(0)
            groups(dve, dve_group, step, 2 * (2 * CH + 3))

            def e_hidden(n, par):
                dve.wait_ge(eg_ready, n + 1)
                tt(eh[par], eg[par], ps[:, 2 + par, :].rearrange("p (s u i) -> p s u i", s=2, u=2)[:, :, 1, :],
                   ALU.mult).then_inc(eh_ready, 1)

            def e_out(n, q):
                dve.wait_ge(ey_ready, n + 1)
                tsc(ey[q][:, 1, :], ps[:, 7, 0:D], rows[q][:, 1, D + 1:D + 2], None, ALU.mult
                    ).then_inc(ey_dve, 1)

            def ehT_copy(n, par):
                dve.wait_ge(ehposed, n + 1)
                nc.vector.tensor_copy(ehT[par], ps[:, 4 + par, 0:2 * P]).then_inc(ehT_ready, 1)

            def dve_pair(n, q):
                e_hidden(n, q % 2)
                e_out(n - 1, (q + RING - 1) % RING)
                ehT_copy(n, q % 2)

            e_hidden(0, 0)
            ehT_copy(0, 0)
            pairs(dve, dve_pair)
            e_out(PAIRS - 1, RING - 1)

            def sum_results(it):
                for q in range(4):
                    s8 = f_sum[q % 2]
                    dve.wait_ge(f_loaded[q], 32 * (it + 1))
                    do(tt(s8, f_y[q][:, 0:4 * D], f_y[q][:, 4 * D:8 * D], ALU.add))
                    do(tt(s8[:, 0:2 * D], s8[:, 0:2 * D], s8[:, 2 * D:4 * D], ALU.add))
                    if not is_(it, 0):
                        dve.wait_ge(f_stored[q], 16 * it)
                    do(tt(f_out[q], s8[:, 0:D], s8[:, D:2 * D], ALU.add))
                    tt(f_out[q], f_out[q], f_part[q], ALU.add).then_inc(f_summed[q], 1)

            sum_results(0)
            with dve.Fori(1, NT // 4) as it:
                step.enter(it - 1, 12)
                sum_results(it)
                step.leave(NT // 4 - 1)

        @block.tensor
        def _(pe):
            mm, tp = nc.tensor.matmul, nc.tensor.transpose

            def a0_transpose(g, par):
                pe.wait_ge(a0_xn_ready, g + 1)
                for c in range(DC):
                    for t in range(GT):
                        last = tp(ps[:, 2 * par + c, t * P:(t + 1) * P], a0_xn[par][:, t, c * P:(c + 1) * P],
                                  ident[:, :])
                last.then_inc(a0_xposed, 1)

            def a0_router(g, par):
                pe.wait_ge(a0_xT_ready, g + 1)
                for t in range(GT):
                    for c in range(DC):
                        last = mm(ps[:, 4 + par, t * E:(t + 1) * E], a0_xT[par][:, c, t * P:(t + 1) * P],
                                  gT[:, c, :], start=c == 0, stop=c == DC - 1)
                last.then_inc(a0_logits_ready, 1)

            pe.wait_ge(consts_made, 1)
            pe.wait_ge(consts_loaded, 16 * CONSTS)
            a0_transpose(0, 0)
            with pe.Fori(0, GROUPS // 2 - 1) as it:
                for par in range(2):
                    a0_transpose(2 * it + par + 1, 1 - par)
                    a0_router(2 * it + par, par)
            a0_transpose(GROUPS - 1, 1)
            a0_router(GROUPS - 2, 0)
            a0_router(GROUPS - 1, 1)

            pe.wait_ge(sel_ready, 1)
            for b in range(4):
                mm(ps[:, b, :], ones_bf[:, :], sel_et[:, 512 * b:512 * (b + 1)], start=True, stop=True)
                last = mm(ps[:, 4 + b, :], before[:, :], sel_et[:, 512 * b:512 * (b + 1)], start=True, stop=True)
            last.then_inc(ranks_ready, 1)

            def transpose_group(n, src, ready, posed):
                pe.wait_ge(ready, n + 1)
                for c in range(DC):
                    for t in range(GT):
                        last = tp(ps[:, c, t * P:(t + 1) * P], src[:, t, c * P:(c + 1) * P], ident[:, :])
                last.then_inc(posed, 1)

            def bu_product(n):
                pe.wait_ge(xT_ready, n + 1)
                for t in range(GT):
                    for c in range(DC):
                        last = mm(ps[:, 0, t * N_STATE:(t + 1) * N_STATE], xT[:, c, t * P:(t + 1) * P],
                                  bT[:, c, :], start=c == 0, stop=c == DC - 1)
                last.then_inc(bu_ready, 1)

            def bu_transpose(n):
                apart(pe, (bu_scaled, n + 1))
                for t in range(GT):
                    last = tp(ps[0:N_STATE, 1, t * P:(t + 1) * P], bu[:, t, :], ident[:, :])
                last.then_inc(buT_ready, 1)

            def y_product(n):
                pe.wait_ge(hs_ready, n + 1)
                for t in range(GT):
                    last = mm(ps[:, t // 2, (t % 2) * D:(t % 2 + 1) * D], hs[:, t * P:(t + 1) * P], cT[:, :],
                              start=True, stop=True)
                last.then_inc(y_ready, 1)

            def gu_product(g, s):
                if not is_(g, 0) or s >= 2:
                    pe.wait_ge(h_made, CH * g + s - 1)
                m = f_rows(s)
                src = xT if s < 2 else zT
                w = shgu if s < 2 else w13
                lo = P * (s if s < 2 else s - 2)
                for u in range(2):
                    for c in range(DC):
                        last = mm(ps[0:m, 2 + 2 * (s % 2) + u, :], w[:, u, c, lo:lo + m], src[:, c, :],
                                  start=c == 0, stop=c == DC - 1)
                last.then_inc(gu_ready, 1)

            def down_product(g):
                pe.wait_ge(h_made, CH * (g + 1))
                if not is_(g, 0):
                    pe.wait_ge(part_ready, g)
                for t in range(GT):
                    for s in range(CH):
                        m = f_rows(s)
                        w = shd[:, s, :] if s < 2 else w2[0:m, s - 2, :]
                        last = mm(ps[:, 6 + t // 2, (t % 2) * D:(t % 2 + 1) * D], h[0:m, s, t * P:(t + 1) * P], w,
                                  start=s == 0, stop=s == CH - 1)
                last.then_inc(down_ready, 1)

            def pe_group(g, par):
                more = not is_(g, GROUPS - 1)
                for s in range(CH):
                    gu_product(g, s)
                    if s == 1:
                        pe.wait_ge(zT_ready, g + 1)
                    if more and s == 1:
                        transpose_group(g + 1, xn, xn_ready, xposed)
                    if more and s == 2:
                        bu_product(g + 1)
                    if more and s == 3:
                        bu_transpose(g + 1)
                    if more and s == 4:
                        y_product(g + 1)
                if more:
                    transpose_group(g + 1, z, z_ready, zposed)
                down_product(g)

            pe.wait_ge(weights_folded, 1)
            pe.wait_ge(routing_done, 1)
            transpose_group(0, xn, xn_ready, xposed)
            bu_product(0)
            bu_transpose(0)
            y_product(0)
            transpose_group(0, z, z_ready, zposed)
            groups(pe, pe_group)

            def r_transpose(n, q):
                pe.wait_ge(rows_loaded[q], 16 // RING * (n - q) + 16)
                for s in range(2):
                    for c in range(DC):
                        j = 2 * s + c
                        last = tp(ps[:, q % 2, j * P:(j + 1) * P], rows[q][:, s, c * P:(c + 1) * P], ident[:, :])
                last.then_inc(rposed, 1)

            def e_gu(n, par, offsets):
                pe.wait_ge(rT_ready, n + 1)
                for s in range(2):
                    for c in range(DC):
                        j = 2 * s + c
                        last = mm(ps[:, 2 + par, s * D:(s + 1) * D], rT[par][:, j * P:(j + 1) * P],
                                  big[:, ds(offsets[s] + c * D, D)], start=c == 0, stop=c == DC - 1)
                last.then_inc(egu_ready, 1)

            def e_transpose(n, par):
                pe.wait_ge(eh_ready, n + 1)
                for s in range(2):
                    last = tp(ps[:, 4 + par, s * P:(s + 1) * P], eh[par][:, s, :], ident[:, :])
                last.then_inc(ehposed, 1)

            def e_down(n, par, offsets):
                pe.wait_ge(ey_act, n)
                pe.wait_ge(ehT_ready, n + 1)
                for s in range(2):
                    last = mm(ps[:, 6 + s, 0:D], ehT[par][:, s * P:(s + 1) * P],
                              big[:, ds(offsets[s] + 2 * D, D)], start=True, stop=True)
                last.then_inc(ey_ready, 1)

            regs = [[pe.alloc_register(f"offset{j}_{k}") for k in range(4)] for j in range(3)]

            def load_offsets(n, first):
                for j in range(first, 3):
                    pe.load(regs[j], te_row[0:1, ds(2 * n + 4 * (j - first) - 4 * (1 - first), 4)])

            def offsets_of(j):
                return [pe.snap(regs[j // 2][2 * (j % 2) + s], min_val=0, max_val=(E - 1) * WEXP) for s in range(2)]

            def pe_pair(n, q):
                e_gu(n, q % 2, offsets_of(q % 4 + 2))
                if not is_(n, PAIRS - 1):
                    r_transpose(n + 1, (q + 1) % RING)
                e_down(n - 1, (q + 1) % 2, offsets_of(q % 4 + 1))
                if q % 4 == 3 and not is_(n, PAIRS - 1):
                    load_offsets(n + 1, 0)
                e_transpose(n, q % 2)

            pe.wait_ge(part_ready, GROUPS)
            r_transpose(0, 0)
            pe.wait_ge(te_loaded, 16)
            pe.wait_ge(wexp_loaded, 16 * (GROUPS + 1))
            load_offsets(0, 1)
            e_gu(0, 0, offsets_of(2))
            r_transpose(1, 1)
            e_transpose(0, 0)
            pairs(pe, pe_pair)
            e_down(PAIRS - 1, 1, offsets_of(5))


def kernel(**inputs):
    import numpy as np
    import concourse.bacc as bacc
    from concourse.bass_utils import run_bass_kernel_spmd

    a = {k.replace("L0_attn_", "").replace("L0_ffn_", "f_"): np.asarray(v) for k, v in inputs.items()}

    def split(m):
        return m.reshape(-1, P, m.shape[1]).transpose(1, 0, 2)

    gu = np.concatenate([a["f_w_gate"], a["f_w_up"]], axis=1).transpose(2, 0, 1)
    gu = gu.reshape(DC, P, E, 2 * INNER).transpose(1, 2, 0, 3).reshape(P, E, DC * 2 * INNER)
    wexp = np.concatenate([gu, a["f_w_down"].transpose(2, 0, 1)], axis=2).reshape(P, E * WEXP)
    arrays = {
        "x": a["x"].reshape(-1, D),
        "log_lambda": a["log_lambda"],
        "BT": split(a["B_w"].T),
        "CT": a["C_w"].T,
        "D_skip": a["D_skip"],
        "ssm_w": a["ssm_norm_w"],
        "ssm_w_col": a["ssm_norm_w"].reshape(DC, P).T,
        "ffn_w_col": a["ffn_norm_w"].reshape(DC, P).T,
        "w13T": np.stack([split(a["w1"].T), split(a["w3"].T)], axis=1),
        "w2T": a["w2"].T,
        "gateT": split(a["f_gate_w"].T),
        "gate_bias": a["f_gate_bias"],
        "wexp": wexp,
        "shguT": np.stack([split(a["f_sh_gate"].T), split(a["f_sh_up"].T)], axis=1),
        "shdT": split(a["f_sh_down"].T),
    }
    nc = bacc.Bacc("TRN2", target_bir_lowering=False, num_devices=1)
    arrays = {f"in_{k}": np.ascontiguousarray(v) for k, v in arrays.items()}
    args = [nc.dram_tensor(k, v.shape, mybir.dt.from_np(v.dtype), kind="ExternalInput").ap()
            for k, v in arrays.items()]
    out = nc.dram_tensor("out", arrays["in_x"].shape, F32, kind="ExternalOutput").ap()
    build(nc, *args, out)
    r = run_bass_kernel_spmd(nc, [arrays], core_ids=[0])
    return r.results[0]["out"].reshape(a["x"].shape)
```

```python
from contextlib import ExitStack

import concourse.bass as bass
from concourse import mybir

P = 128
F32 = mybir.dt.float32
BF16 = mybir.dt.bfloat16
U32 = mybir.dt.uint32
ALU = mybir.AluOpType
ACT = mybir.ActivationFunctionType
AX_X = mybir.AxisListType.X
ds = bass.ds

D = 256
DC = D // P
N_STATE = 64
D_FF = 688
FT = -(-D_FF // P)
E = 32
NG = 8
EG = E // NG
TOP_GROUPS = 4
K = 8
INNER = 128
SHARED = 256
ROUTE_SCALE = 2.5
LN_EPS = 1e-5
RMS_EPS = 1e-6
ACCS = 4
ROW = D + 2
WEXP = 3 * D
GT = 4
G = GT * P


def is_(i, n):
    return isinstance(i, int) and i == n


class Steps:

    def __init__(self, eng, sem):
        self.eng, self.sem, self.base, self.n = eng, sem, 0, 0

    def done(self, ins):
        ins.then_inc(self.sem, 1)
        self.n += 1

    def wait(self):
        self.eng.wait_ge(self.sem, self.base + self.n)

    def enter(self, i, per):
        self.start = (self.base, self.n, per)
        self.base, self.n = self.base + self.n + i * per, 0

    def leave(self, count):
        base, n, per = self.start
        assert self.n == per, (self.n, per)
        self.base, self.n = base + n + count * per, 0


def build(nc, x, log_lambda, BT, CT, D_skip, ssm_w, ssm_w_col, ffn_w_col, w13T, w2T, gateT, gate_bias, wexp,
          shguT, shdT, out):
    T = x.shape[0]
    NT = T // P
    GROUPS = T // G
    NTILE = T * K // P + E
    NSLOT = NTILE * P
    PAIRS = NTILE // 2
    RING = 8
    CH = FT + SHARED // P
    TE_C = -(-NTILE // P)
    W = NT * E
    FIRST = 2
    BATCH = 5
    LAST = FIRST + NT // BATCH
    FW = 2 * D
    FN = T * D // (P * FW)
    assert LAST == GROUPS - 2 and GROUPS == 16 and PAIRS % RING == 0 and NT % 4 == 0

    sorted_rows = nc.dram_tensor("sorted_rows", [NSLOT + P, ROW], F32).ap()
    accs = [nc.dram_tensor(f"acc{a}", [T + P, D], F32).ap() for a in range(ACCS)]
    tile_expert_dram = nc.dram_tensor("tile_expert_dram", [P * TE_C], U32).ap()

    with ExitStack() as ctx:
        def sb(name, shape, dt=F32):
            return ctx.enter_context(nc.sbuf_tensor(name, shape, dt))

        def sem(name):
            return ctx.enter_context(nc.semaphore(name))

        big = sb("big", [P, E * WEXP])
        xs = big[:, 0:NT * D].rearrange("p (t d) -> p t d", d=D)
        tables = big[:, NT * D:NT * D + 3 * W].rearrange("p (k n) -> p k n", k=3)
        order_te = tables[:, 0, :].rearrange("p (t e) -> p t e", e=E)
        weight_te = tables[:, 1, :].rearrange("p (t e) -> p t e", e=E)
        slot_te = tables[:, 2, :].rearrange("p (t e) -> p t e", e=E)

        w13 = sb("w13", [P, 2, DC, D_FF])
        w2 = sb("w2", [P, FT, D])
        shgu = sb("shgu", [P, 2, DC, SHARED])
        shd = sb("shd", [P, SHARED // P, D])
        bT = sb("bT", [P, DC, N_STATE])
        cT = sb("cT", [N_STATE, D])
        gT = sb("gT", [P, DC, E])
        skip_w = sb("skip_w", [P, D])
        ssmw_row = sb("ssmw_row", [P, D])
        ssmw_col = sb("ssmw_col", [P, DC])
        ffnw_col = sb("ffnw_col", [P, DC])
        bias_row = sb("bias_row", [P, E])
        loglam = sb("loglam", [N_STATE, 1])
        lam = sb("lam", [N_STATE, 1])
        ident = sb("ident", [P, P])
        before = sb("before", [P, P], BF16)
        ones_bf = sb("ones_bf", [P, P], BF16)
        codes = sb("codes", [P, NT], U32)
        order_c = sb("order_c", [P, K])
        ln_eps = sb("ln_eps", [P, 1])
        rms_eps = sb("rms_eps", [P, 1])
        stage = sb("stage", [P, K, ROW])
        stage_idx = sb("stage_idx", [P, K], U32)
        meta = sb("meta", [P, 3, K // 2, E])
        eq, eq_w, eq_s = (meta[:, j, :, :] for j in range(3))
        pad_row = sb("pad_row", [P, ROW])
        pad_starts = sb("pad_starts", [P, E], U32)
        bn6 = sb("bn6", [P, 2, GT, 6])
        mv4 = sb("mv4", [P, 2, GT, 2])
        mv = sb("mv", [P, NT, 2])
        rstd = sb("rstd", [P, NT])
        nmr = sb("nmr", [P, NT])
        rinv = sb("rinv", [P, NT])
        ssz = sb("ssz", [P, GT])
        rz = sb("rz", [P, GT])
        te_u = sb("te_u", [P, TE_C], U32)
        te_row = sb("te_row", [1, P * TE_C], U32)

        arena = sb("arena", [P, 13824])
        at = [0]

        def take(n):
            at[0] += n
            assert at[0] <= 13824
            return arena[:, at[0] - n:at[0]]

        xn = take(GT * D).rearrange("p (t d) -> p t d", d=D)
        xT = take(DC * G).rearrange("p (c n) -> p c n", c=DC)
        bu = take(GT * N_STATE).rearrange("p (t n) -> p t n", n=N_STATE)
        hs = take(G)[0:N_STATE, :]
        lam_b = take(G)[0:N_STATE, :]
        x1 = take(GT * D).rearrange("p (t d) -> p t d", d=D)
        z = take(GT * D).rearrange("p (t d) -> p t d", d=D)
        at_zT = at[0]
        zT = take(DC * G).rearrange("p (c n) -> p c n", c=DC)
        at_h = at[0]
        h = take(CH * G).rearrange("p (f n) -> p f n", n=G)
        gate = [take(G) for _ in range(2)]
        at_part = at[0]
        part = [take(GT * D).rearrange("p (t d) -> p t d", d=D) for _ in range(2)]
        at[0] = at_h
        a0_xn = [take(GT * D).rearrange("p (t d) -> p t d", d=D) for _ in range(2)]
        a0_xT = [take(DC * G).rearrange("p (c n) -> p c n", c=DC) for _ in range(2)]
        a0_lT = [take(G)[0:E, :] for _ in range(2)]
        assert at[0] <= at_part
        spare = big[:, NT * D + 3 * W:]
        sel_et = spare[:, 0:W // 2].bitcast(BF16)
        restart_te = spare[:, W // 2:W].bitcast(BF16)
        restart_et = sb("restart_et", [P, 512], BF16)
        work = stage[:, :, :].rearrange("p k w -> p (k w)")[:, 0:W]
        sel = sb("sel", [P, W])[:, :]
        logits, masked = tables[:, 0, :], tables[:, 0, :]
        scores = tables[:, 1, :]
        sc = tables[:, 2, :]
        repl = work
        masked_te, repl_te, sel_te, work_te = (
            a.rearrange("p (t e) -> p t e", e=E) for a in (masked, repl, sel, work))
        scores_te = scores.rearrange("p (t e) -> p t e", e=E)
        hi01, lo01, hi23, lo23 = (work[:, k * NT * NG:(k + 1) * NT * NG] for k in range(4))
        gs, rank, beats = (sel[:, k * NT * NG:(k + 1) * NT * NG] for k in range(3))
        gs_tg, rank_tg, beats_tg = (a.rearrange("p (t g) -> p t g", g=NG) for a in (gs, rank, beats))
        flat_meta = meta[:, :, :, :].rearrange("p a k e -> p (a k e)")
        ne, ntf, endt, base, nt_f, ones_e, full_f = (flat_meta[:, j * E:(j + 1) * E] for j in range(7))
        nt_u, full_u = nt_f.bitcast(U32), full_f.bitcast(U32)
        full = flat_meta[:, 7 * E:8 * E]
        den = flat_meta[:, 8 * E:8 * E + NT]
        te_cmp = sel[:, 0:TE_C * E].rearrange("p (c e) -> p c e", e=E)
        te_f = sel[:, TE_C * E:TE_C * E + TE_C]
        tile_i = sb("tile_i", [P, TE_C], U32)
        tile_f = sb("tile_f", [P, TE_C])
        max8 = sb("max8", [P, 2, GT * 2, K])
        at[0] = 0
        rows = [take(2 * ROW).rearrange("p (s w) -> p s w", w=ROW) for _ in range(RING)]
        rT = [take(2 * D) for _ in range(2)]
        assert at[0] <= at_zT
        at[0] = at_zT
        eg = [take(2 * INNER).rearrange("p (s i) -> p s i", i=INNER) for _ in range(2)]
        eh = [take(2 * INNER).rearrange("p (s i) -> p s i", i=INNER) for _ in range(2)]
        assert at[0] <= at_h
        at[0] = at_h
        ehT = [take(2 * P) for _ in range(2)]
        ey = [take(2 * D).rearrange("p (s d) -> p s d", d=D) for _ in range(RING)]
        assert at[0] <= at_part
        at[0] = 0
        f_in = [[big[:, (ACCS * q + a) * FW:(ACCS * q + a + 1) * FW] for a in range(ACCS)] for q in range(4)]
        f_out = [take(FW) for _ in range(4)]

        ps = ctx.enter_context(nc.psum_tensor("ps", [P, 8, 512], F32))

        x_loaded = [sem(f"x_loaded{j}") for j in range(4)]
        router_loaded = sem("router_loaded")
        consts_loaded = sem("consts_loaded")
        consts_made = sem("consts_made")
        pool_step = sem("pool_step")
        dve_step = sem("dve_step")
        act_step = sem("act_step")
        var_ready = sem("var_ready")
        std_ready = sem("std_ready")
        nmr_ready = sem("nmr_ready")
        a0_xn_dve = sem("a0_xn_dve")
        a0_xn_act = sem("a0_xn_act")
        a0_xposed = sem("a0_xposed")
        a0_xT_ready = sem("a0_xT_ready")
        a0_products_ready = sem("a0_products_ready")
        a0_lT_ready = sem("a0_lT_ready")
        a0_logits_ready = sem("a0_logits_ready")
        logits_kept = sem("logits_kept")
        ms_x_ready = sem("ms_x_ready")
        scores_ready = sem("scores_ready")
        rms_x_ready = sem("rms_x_ready")
        bT_folded = sem("bT_folded")
        w13_folded = sem("w13_folded")
        sel_ready = sem("sel_ready")
        sel_et_ready = sem("sel_et_ready")
        starts_ready = sem("starts_ready")
        padded = sem("padded")
        padded_by_pool = sem("padded_by_pool")
        accs_zeroed = sem("accs_zeroed")
        ranks_used = sem("ranks_used")
        ranks_ready = sem("ranks_ready")
        routing_done = sem("routing_done")
        te_ready = sem("te_ready")
        te_stored = sem("te_stored")
        te_loaded = sem("te_loaded")
        lam_ready = sem("lam_ready")

        xn_ready = sem("xn_ready")
        xposed = sem("xposed")
        xT_ready = sem("xT_ready")
        bu_ready = sem("bu_ready")
        bu_scaled = sem("bu_scaled")
        buT_ready = sem("buT_ready")
        hs_ready = sem("hs_ready")
        y_ready = sem("y_ready")
        x1_ready = sem("x1_ready")
        rms_z_ready = sem("rms_z_ready")
        z_ready = sem("z_ready")
        zposed = sem("zposed")
        zT_ready = sem("zT_ready")
        gu_ready = sem("gu_ready")
        gate_ready = sem("gate_ready")
        h_made = sem("h_made")
        down_ready = sem("down_ready")
        part_ready = sem("part_ready")
        part_stored = [sem(f"part_stored{j}") for j in range(2)]
        stage_x = [sem(f"stage_x{j}") for j in range(2)]
        stage_meta = [sem(f"stage_meta{j}") for j in range(2)]
        scattered = [sem(f"scattered{j}") for j in range(2)]
        wexp_loaded = sem("wexp_loaded")

        rows_loaded = [sem(f"rows_loaded{j}") for j in range(RING)]
        rposed = sem("rposed")
        rT_ready = sem("rT_ready")
        egu_ready = sem("egu_ready")
        eg_ready = sem("eg_ready")
        eh_ready = sem("eh_ready")
        ehposed = sem("ehposed")
        ehT_ready = sem("ehT_ready")
        ey_ready = sem("ey_ready")
        ey_act = sem("ey_act")
        ey_dve = sem("ey_dve")
        ey_stored = [sem(f"ey_stored{j}") for j in range(RING)]
        f_loaded = [sem(f"f_loaded{j}") for j in range(4)]
        f_summed = [sem(f"f_summed{j}") for j in range(4)]
        f_stored = [sem(f"f_stored{j}") for j in range(4)]

        block = ctx.enter_context(nc.Block())

        CONSTS = 13

        def f_rows(s):
            return P if s < CH - 1 else D_FF - (FT - 1) * P

        HALVES = {0: [0], 1: [1], 3: [2], 4: [3], 5: [4], 6: [5], 7: [6]}
        LATE_HALVES = [7, 8, 9]

        def staged(g, halves):
            if isinstance(g, int) and not FIRST <= g <= LAST:
                return []
            return [((g - FIRST) * BATCH + i // 2, i % 2) for i in halves
                    if not is_(g, LAST) or i // 2 < NT % BATCH]

        def apart(eng, *waits):
            values = [v if isinstance(v, int) else eng.to_reg(v) for _, v in waits]
            eng.wait_ge(consts_made, 1)
            for (s, _), v in zip(waits, values):
                eng.wait_ge(s, v)

        def groups(eng, body, step=None, per=0):
            for g in range(3):
                body(g, g % 2)
            with eng.Fori(0, (GROUPS - 6) // 2) as it:
                if step:
                    step.enter(it, per)
                for j in range(2):
                    body(2 * it + 3 + j, 1 - j)
                if step:
                    step.leave((GROUPS - 6) // 2)
            for g in range(GROUPS - 3, GROUPS):
                body(g, g % 2)

        LEAD = 3

        def exists(g):
            return not isinstance(g, int) or 0 <= g < GROUPS

        def a0_groups(eng, body, step=None, per=0):
            for g in range(-LEAD, 4):
                body(g, g % 4)
            with eng.Fori(1, GROUPS // 4 - 1) as it:
                if step:
                    step.enter(it - 1, per)
                for j in range(4):
                    body(4 * it + j, j)
                if step:
                    step.leave(GROUPS // 4 - 2)
            for g in range(GROUPS - 4, GROUPS):
                body(g, g % 4)

        def first_apart(eng, count, body):
            body(0)
            with eng.Fori(1, count) as i:
                body(i)

        def pairs(eng, body):
            for n in range(1, RING):
                body(n, n)
            with eng.Fori(0, PAIRS // RING - 2) as it:
                for q in range(RING):
                    body(RING * it + RING + q, q)
            for q in range(RING):
                body(PAIRS - RING + q, q)

        def store_padding(eng, half, done):
            eng.wait_ge(starts_ready, 1)
            eng.wait_ge(padded, 16)
            with eng.Fori(0, E // 2) as e:
                start = eng.value_load(pad_starts[0:1, ds(e + half * (E // 2), 1)], min_val=0, max_val=NSLOT)
                eng.dma_start(sorted_rows[ds(start, P), :], pad_row[:, :]).then_inc(done, 16)

        @block.sync
        def _(sp):
            def load_x(it):
                for j in range(4):
                    if not is_(it, 0):
                        sp.wait_ge(x_loaded[j], 16 * it)
                    sp.dma_start(xs[:, ds((4 * it + j) * GT, GT), :],
                                 x[ds((4 * it + j) * G, G), :].rearrange("(t p) d -> p t d", p=P)
                                 ).then_inc(x_loaded[j], 16)

            load_x(0)
            for dst, src in ((bT[:, :, :], BT), (ssmw_col[:, :], ssm_w_col),
                             (skip_w[:, :], D_skip.partition_broadcast(P)),
                             (ssmw_row[:, :], ssm_w.partition_broadcast(P)),
                             (loglam[:, :], log_lambda.rearrange("(n a) -> n a", a=1)),
                             (bias_row[:, :], gate_bias.partition_broadcast(P)),
                             (cT[:, :], CT), (ffnw_col[:, :], ffn_w_col),
                             (shgu[:, :, :, :], shguT), (w13[:, :, :, :], w13T),
                             (w2[:, 0:FT - 1, :], w2T[0:(FT - 1) * P, :].rearrange("(f p) d -> p f d", p=P)),
                             (w2[0:D_FF - (FT - 1) * P, FT - 1, :], w2T[(FT - 1) * P:, :]),
                             (shd[:, :, :], shdT)):
                sp.dma_start(dst, src).then_inc(consts_loaded, 16)
            with sp.Fori(1, GROUPS // 4) as it:
                load_x(it)
            sp.wait_ge(consts_made, 1)
            sp.dma_start(sorted_rows[T * K:NSLOT, :].rearrange("(t p) w -> p t w", p=P),
                         pad_row[:, :].unsqueeze(1).to_broadcast([P, E, ROW])).then_inc(padded, 16)
            for acc in accs:
                sp.dma_start(acc[T:, :], pad_row[:, 0:D]).then_inc(accs_zeroed, 16)

            def zero_accs(g):
                for a in range(1, ACCS):
                    sp.wait_ge(h_made, CH * g + 2 * a)
                    sp.dma_start(accs[a][ds(g * G, G), :].rearrange("(t p) d -> p t d", p=P),
                                 pad_row[:, 0:D].unsqueeze(1).to_broadcast([P, GT, D])).then_inc(accs_zeroed, 16)

            def turn_tile_experts():
                sp.wait_ge(te_ready, 1)
                sp.dma_start(tile_expert_dram.rearrange("(p c) -> p c", c=TE_C), te_u[:, :]).then_inc(te_stored, 16)
                sp.wait_ge(te_stored, 16)
                sp.dma_start(te_row[:, :], tile_expert_dram.rearrange("(a n) -> a n", a=1)).then_inc(te_loaded, 16)
            def store_part(g, par):
                zero_accs(g)
                if is_(g, 1):
                    store_padding(sp, 0, padded)
                sp.wait_ge(part_ready, g + 1)
                sp.dma_start(accs[0][ds(g * G, G), :].rearrange("(t p) d -> p t d", p=P), part[par]
                             ).then_inc(part_stored[par], 16)
                if is_(g, 1):
                    turn_tile_experts()
                if is_(g, LAST):
                    sp.wait_ge(stage_x[1], NT)
                    lo = (LAST - FIRST) * BATCH * D
                    sp.dma_start(big[:, lo:], wexp[:, lo:]).then_inc(wexp_loaded, 16)
                elif not isinstance(g, int) or FIRST <= g < LAST:
                    sp.wait_ge(stage_x[1], BATCH * (g + (1 - FIRST)))
                    sp.dma_start(big[:, ds((g - FIRST) * BATCH * D, BATCH * D)],
                                 wexp[:, ds((g - FIRST) * BATCH * D, BATCH * D)]).then_inc(wexp_loaded, 16)

            groups(sp, store_part)
            sp.wait_ge(scattered[0], 16 * (K // 2) * NT)
            sp.wait_ge(scattered[1], 16 * (K // 2) * NT)
            sp.wait_ge(h_made, CH * GROUPS)

            def load_rows(it):
                for q in range(RING):
                    if not is_(it, 0):
                        sp.wait_ge(ey_stored[q], 32 * it)
                    sp.dma_start(rows[q], sorted_rows[ds((RING * it + q) * 2 * P, 2 * P), :]
                                 .rearrange("(s p) w -> p s w", p=P)).then_inc(rows_loaded[q], 16)

            first_apart(sp, PAIRS // RING, load_rows)
            for q in range(RING):
                sp.wait_ge(ey_stored[q], 32 * (PAIRS // RING))

            def load_sums(it):
                for q in range(4):
                    if not is_(it, 0):
                        sp.wait_ge(f_summed[q], it)
                    for a in range(ACCS):
                        sp.dma_start(f_in[q][a], accs[a][ds((4 * it + q) * (T // FN), T // FN), :]
                                     .rearrange("(p k) d -> p (k d)", p=P)).then_inc(f_loaded[q], 16)

            first_apart(sp, FN // 4, load_sums)

        @block.gpsimd
        def _(pool):
            step = Steps(pool, pool_step)
            step.done(nc.gpsimd.memset(ident[:, :], 0.0))
            step.done(nc.gpsimd.memset(before[:, :], 1.0))
            nc.gpsimd.memset(ones_bf[:, :], 1.0)
            for k in range(K):
                nc.gpsimd.memset(order_c[:, k:k + 1], float(k - 100))
            nc.gpsimd.memset(ln_eps[:, :], LN_EPS)
            nc.gpsimd.memset(rms_eps[:, :], RMS_EPS)
            step.done(nc.gpsimd.memset(pad_row[:, :], 0.0))
            nc.gpsimd.iota(codes[:, :], pattern=[[P, NT]], base=0, channel_multiplier=1)
            step.done(nc.gpsimd.memset(restart_te, 1.0))
            step.done(nc.gpsimd.memset(restart_et[:, :], 1.0))
            nc.gpsimd.iota(tile_i[:, :], pattern=[[1, TE_C]], base=0, channel_multiplier=TE_C)
            step.wait()
            nc.gpsimd.affine_select(out=ident[:, :], in_=ident[:, :], compare_op=ALU.not_equal, fill=1.0, base=0,
                                    pattern=[[-1, P]], channel_multiplier=1)
            nc.gpsimd.affine_select(out=before[:, :], in_=before[:, :], compare_op=ALU.is_gt, fill=0.0, base=0,
                                    pattern=[[1, P]], channel_multiplier=-1)
            nc.gpsimd.memset(restart_te.rearrange("p (t e) -> p t e", e=E)[:, :, 0:1], 0.0)
            nc.gpsimd.memset(restart_et[:, :].rearrange("p (e t) -> p e t", t=NT)[:, :, 0:1], 0.0)
            nc.gpsimd.iota(pad_row[:, D:D + 1].bitcast(U32), pattern=[[0, 1]], base=T, channel_multiplier=1
                           ).then_inc(consts_made, 1)
            store_padding(pool, 1, padded_by_pool)
            pool.wait_ge(padded_by_pool, 16 * (E // 2))
            pool.wait_ge(padded, 16 * (E // 2 + 1))

            def scatter_tile(i):
                for half in range(2):
                    apart(pool, (stage_x[half], i + 1), (stage_meta[half], i + 1))
                    for k in range(K // 2 * half, K // 2 * (half + 1)):
                        pool.indirect_dma_start(
                            out=sorted_rows, out_offset=bass.IndirectOffsetOnAxis(ap=stage_idx[:, k:k + 1], axis=0),
                            in_=stage[:, k, :], in_offset=None).then_inc(scattered[half], 16)

            first_apart(pool, NT, scatter_tile)

            pool.wait_ge(accs_zeroed, 16 * (ACCS + (ACCS - 1) * GROUPS))
            pool.wait_ge(part_stored[0], 16 * GROUPS // 2)
            pool.wait_ge(part_stored[1], 16 * GROUPS // 2)

            def add_results(it):
                for q in range(RING):
                    waits = [(ey_act, RING * it + (q + 1)), (ey_dve, RING * it + (q + 1))]
                    if q >= 2:
                        waits.append((ey_stored[q - 2], 32 * it + 32))
                    elif not is_(it, 0):
                        waits.append((ey_stored[q + RING - 2], 32 * it))
                    apart(pool, *waits)
                    for s in range(2):
                        pool.indirect_dma_start(
                            out=accs[(2 * q + s) % ACCS],
                            out_offset=bass.IndirectOffsetOnAxis(ap=rows[q].bitcast(U32)[:, s, D:D + 1], axis=0),
                            in_=ey[q][:, s, :], in_offset=None, compute_op=ALU.add).then_inc(ey_stored[q], 16)

            first_apart(pool, PAIRS // RING, add_results)

        @block.scalar
        def _(act):
            step = Steps(act, act_step)
            act.dma_start(gT[:, :, :], gateT).then_inc(router_loaded, 16)
            act.wait_ge(consts_made, 1)

            def a0_std(g):
                act.wait_ge(var_ready, g + 1)
                nc.scalar.activation(rstd[:, ds(g * GT, GT)], mv[:, ds(g * GT, GT), 1], ACT.Sqrt, bias=ln_eps[:, :]
                                     ).then_inc(std_ready, 1)

            def a0_normalise(g, par):
                apart(act, (nmr_ready, g + 1))
                for t in range(GT // 2, GT):
                    i = g * GT + t
                    last = nc.scalar.activation(a0_xn[par][:, t, :], xs[:, ds(i, 1), :].rearrange("p t d -> p (t d)"),
                                                ACT.Identity, bias=nmr[:, ds(i, 1)], scale=rstd[:, ds(i, 1)])
                last.then_inc(a0_xn_act, 1)

            def a0_copy(g, par):
                act.wait_ge(a0_xposed, g + 1)
                for c in range(DC):
                    last = nc.scalar.activation(a0_xT[par][:, c, :], ps[:, 2 * par + c, :], ACT.Copy)
                last.then_inc(a0_xT_ready, 1)

            def a0_copy_products(g, par):
                act.wait_ge(a0_products_ready, g + 1)
                nc.scalar.activation(a0_lT[par], ps[0:E, 4 + par, :], ACT.Copy).then_inc(a0_lT_ready, 1)

            def a0_keep_logits(g, par):
                act.wait_ge(a0_logits_ready, g + 1)
                nc.scalar.activation(logits[:, ds(g * GT * E, GT * E)], ps[:, 6 + par, 0:GT * E], ACT.Copy
                                     ).then_inc(logits_kept, 1)

            def act_a0(g, j):
                if exists(g + 1):
                    a0_copy(g + 1, (j + 1) % 2)
                if exists(g + 3):
                    a0_std(g + 3)
                if exists(g):
                    a0_copy_products(g, j % 2)
                if exists(g + 2):
                    a0_normalise(g + 2, j % 2)
                if exists(g - 1):
                    a0_keep_logits(g - 1, (j + 1) % 2)

            a0_groups(act, act_a0)
            act.wait_ge(ms_x_ready, 1)
            nc.scalar.activation(rinv[:, :], rinv[:, :], ACT.Sqrt, bias=rms_eps[:, :]).then_inc(rms_x_ready, 1)
            a0_keep_logits(GROUPS - 1, 1)

            def xT_copy(n):
                act.wait_ge(xposed, n + 1)
                for c in range(DC):
                    last = nc.scalar.activation(xT[:, c, :], ps[:, c, :], ACT.Copy)
                last.then_inc(xT_ready, 1)

            def rms_z(n):
                act.wait_ge(x1_ready, n + 1)
                for t in range(GT):
                    last = nc.scalar.activation(z[:, t, :], x1[:, t, :], ACT.Square, accum_out=ssz[:, t:t + 1])
                step.done(last)
                step.wait()
                nc.scalar.activation(ssz[:, :], ssz[:, :], ACT.Sqrt, bias=rms_eps[:, :], scale=1.0 / D
                                     ).then_inc(rms_z_ready, 1)

            def zT_copy(n):
                act.wait_ge(zposed, n + 1)
                for c in range(DC):
                    last = nc.scalar.activation(zT[:, c, :], ps[:, c, :], ACT.Copy)
                last.then_inc(zT_ready, 1)

            def gate_tile(g, s):
                act.wait_ge(gu_ready, CH * g + s + 1)
                if not is_(g, 0) or s >= 2:
                    act.wait_ge(h_made, CH * g + s - 1)
                m = f_rows(s)
                nc.scalar.activation(gate[s % 2][0:m, :], ps[0:m, 2 + 2 * (s % 2), :], ACT.Silu
                                     ).then_inc(gate_ready, 1)

            def stage_half(i, half):
                if is_(i, 0):
                    act.wait_ge(routing_done, 1)
                else:
                    apart(act, (scattered[half], 16 * (K // 2) * i))
                nc.scalar.activation(stage[:, K // 2 * half:K // 2 * (half + 1), 0:D],
                                     xs[:, ds(i, 1), :].to_broadcast([P, K // 2, D]), ACT.Identity,
                                     bias=nmr[:, ds(i, 1)], scale=rstd[:, ds(i, 1)]).then_inc(stage_x[half], 1)

            def act_group(g, par):
                more = not is_(g, GROUPS - 1)
                for s in range(CH):
                    if not is_(g, 0) or s >= 2:
                        gate_tile(g, s)
                    if more and s == CH - 1:
                        rms_z(g + 1)
                    if more and s == 1:
                        xT_copy(g + 1)
                    for i, half in staged(g, HALVES.get(s, [])):
                        stage_half(i, half)
                    if is_(g, 1) and s == 0:
                        act.wait_ge(sel_ready, 1)
                        nc.scalar.activation(sel_et.rearrange("p (e t) -> p t e", t=NT), sel_te, ACT.Copy
                                             ).then_inc(sel_et_ready, 1)
                for i, half in staged(g, LATE_HALVES):
                    stage_half(i, half)
                if more:
                    zT_copy(g + 1)

            xT_copy(0)
            act.wait_ge(consts_loaded, 16 * CONSTS)
            nc.scalar.activation(lam[:, :], loglam[:, :], ACT.Sigmoid).then_inc(lam_ready, 1)
            act.wait_ge(logits_kept, GROUPS)
            nc.scalar.activation(scores, logits, ACT.Sigmoid).then_inc(scores_ready, 1)
            gate_tile(0, 0)
            gate_tile(0, 1)
            rms_z(0)
            zT_copy(0)
            groups(act, act_group, step, 2)

            def rT_copy(n, par):
                act.wait_ge(rposed, n + 1)
                nc.scalar.activation(rT[par], ps[:, par, :], ACT.Copy).then_inc(rT_ready, 1)

            def e_gate(n, par):
                act.wait_ge(egu_ready, n + 1)
                nc.scalar.activation(
                    eg[par], ps[:, 2 + par, :].rearrange("p (s u i) -> p s u i", s=2, u=2)[:, :, 0, :], ACT.Silu
                ).then_inc(eg_ready, 1)

            def e_out(n, q):
                act.wait_ge(ey_ready, n + 1)
                nc.scalar.activation(ey[q][:, 0, :], ps[:, 6, 0:D], ACT.Copy, scale=rows[q][:, 0, D + 1:D + 2]
                                     ).then_inc(ey_act, 1)

            def act_pair(n, q):
                e_gate(n, q % 2)
                if not is_(n, PAIRS - 1):
                    rT_copy(n + 1, (q + 1) % 2)
                e_out(n - 1, (q + RING - 1) % RING)

            rT_copy(0, 0)
            e_gate(0, 0)
            rT_copy(1, 1)
            pairs(act, act_pair)
            e_out(PAIRS - 1, RING - 1)

            with act.Fori(0, FN // 4) as it:
                for q in range(4):
                    act.wait_ge(f_summed[q], it + 1)
                    act.dma_start(out[ds((4 * it + q) * (T // FN), T // FN), :].rearrange("(p k) d -> p (k d)", p=P),
                                  f_out[q]).then_inc(f_stored[q], 16)
            for q in range(4):
                act.wait_ge(f_stored[q], 16 * (FN // 4))

        @block.vector
        def _(dve):
            step = Steps(dve, dve_step)
            tt, tsc = nc.vector.tensor_tensor, nc.vector.tensor_scalar

            def do(ins):
                step.done(ins)
                step.wait()

            def a0_stats(g, j):
                dve.wait_ge(x_loaded[j], 16 * (g // 4 + 1) if isinstance(g, int) else 4 * (g - j) + 16)
                for t in range(GT):
                    last = nc.vector.bn_stats(bn6[:, j % 2, t, :], xs[:, ds(g * GT + t, 1), :]
                                              .rearrange("p t d -> p (t d)"))
                step.done(last)
                apart(dve, (dve_step, step.base + step.n))
                for t in range(GT):
                    last = nc.vector.bn_aggr(mv4[:, j % 2, t, :], bn6[:, j % 2, t, :])
                do(last)
                nc.vector.tensor_copy(mv[:, ds(g * GT, GT), :], mv4[:, j % 2, :, :]).then_inc(var_ready, 1)

            def normalise(dst, g, tiles):
                for t in range(tiles):
                    i = g * GT + t
                    last = tsc(dst[:, t, :], xs[:, ds(i, 1), :].rearrange("p t d -> p (t d)"),
                               rstd[:, ds(i, 1)], nmr[:, ds(i, 1)], ALU.mult, ALU.add)
                return last

            def a0_normalise(g, par):
                of_g = ds(g * GT, GT)
                dve.wait_ge(std_ready, g + 1)
                do(nc.vector.reciprocal(rstd[:, of_g], rstd[:, of_g]))
                do(nc.vector.scalar_tensor_tensor(nmr[:, of_g], mv[:, of_g, 0], -1.0, rstd[:, of_g],
                                                  ALU.mult, ALU.mult))
                dve.sem_inc(nmr_ready, 1)
                if not isinstance(g, int) or g >= 2:
                    dve.wait_ge(a0_xposed, g - 1)
                normalise(a0_xn[par], g, GT // 2).then_inc(a0_xn_dve, 1)

            def dve_a0(g, j):
                if exists(g + 3):
                    a0_stats(g + 3, (j + 3) % 4)
                if exists(g + 2):
                    a0_normalise(g + 2, j % 2)

            a0_groups(dve, dve_a0, step, 16)

            def r_pairs():
                dve.wait_ge(scores_ready, 1)
                do(tt(sc.rearrange("p (t e) -> p t e", e=E), scores_te,
                      bias_row[:, :].unsqueeze(1).to_broadcast([P, NT, E]), ALU.add))
                v = [sc.rearrange("p (n j) -> p n j", j=EG)[:, :, j] for j in range(EG)]
                tt(hi01, v[0], v[1], ALU.max)
                tt(lo01, v[0], v[1], ALU.min)
                tt(hi23, v[2], v[3], ALU.max)
                do(tt(lo23, v[2], v[3], ALU.min))

            def r_groups():
                tt(gs, hi01, hi23, ALU.max)
                do(tt(lo01, lo01, lo23, ALU.max))
                do(tt(hi01, hi01, hi23, ALU.min))
                do(tt(hi01, hi01, lo01, ALU.max))
                do(tt(gs, gs, hi01, ALU.add))
                for g in range(NG):
                    last = nc.vector.memset(rank_tg[:, :, g:g + 1], float(NG - 1 - g))
                do(last)

            def r_ranks(s):
                do(tt(beats_tg[:, :, 0:NG - s], gs_tg[:, :, 0:NG - s], gs_tg[:, :, s:NG], ALU.is_ge))
                do(tt(rank_tg[:, :, s:NG], rank_tg[:, :, s:NG], beats_tg[:, :, 0:NG - s], ALU.add))
                do(tt(rank_tg[:, :, 0:NG - s], rank_tg[:, :, 0:NG - s], beats_tg[:, :, 0:NG - s], ALU.subtract))

            def r_mask():
                do(tsc(beats, rank, float(TOP_GROUPS), None, ALU.is_lt))
                do(tt(masked.rearrange("p (n j) -> p n j", j=EG), sc.rearrange("p (n j) -> p n j", j=EG),
                      beats.unsqueeze(2).to_broadcast([P, NT * NG, EG]), ALU.mult))

            def r_top8(s):
                for j in range(2 * GT):
                    last = nc.vector.max(max8[:, s % 2, j, :], masked_te[:, 2 * GT * s + j, :])
                do(last)
                for j in range(2 * GT):
                    t = 2 * GT * s + j
                    last = nc.vector.match_replace(repl_te[:, t, :], max8[:, s % 2, j, :], masked_te[:, t, :], -1e30)
                step.done(last)

            def r_select():
                step.wait()
                tt(sel, repl, masked, ALU.not_equal).then_inc(sel_ready, 1)

            def r_order():
                dve.wait_ge(sel_ready, 1)
                do(nc.vector.tensor_tensor_scan(work, restart_te, sel, 0.0, ALU.mult, ALU.add))
                do(nc.vector.scalar_tensor_tensor(order_te, sel_te, -101.0, work_te, ALU.mult, ALU.add))

            def r_slots(b):
                r = slice(512 * b, 512 * (b + 1))
                dve.wait_ge(ranks_ready, b + 1)
                do(nc.vector.tensor_tensor_scan(work[:, r], restart_et[:, :], ps[:, 6, :], 0.0, ALU.mult, ALU.add))
                do(nc.vector.tensor_copy(ne[:, b * 512 // NT:(b + 1) * 512 // NT],
                                         work[:, r].rearrange("p (e t) -> p e t", t=NT)[:, :, NT - 1]))
                do(tt(work[:, r], work[:, r], ps[:, 6, :], ALU.subtract))
                tt(work[:, r], work[:, r], ps[:, 7, :], ALU.add).then_inc(ranks_used, 1)

            def r_bases():
                dve.wait_ge(ranks_used, 4)
                tsc(nt_u, ne, float(P - 1), None, ALU.add)
                do(nc.vector.tensor_copy(full_u, ne))
                tsc(nt_u, nt_u, P.bit_length() - 1, None, ALU.logical_shift_right)
                do(tsc(full_u, full_u, P.bit_length() - 1, None, ALU.logical_shift_right))
                nc.vector.memset(ones_e, 1.0)
                nc.vector.tensor_copy(full, full_u)
                do(nc.vector.tensor_copy(ntf, nt_u))
                do(nc.vector.tensor_tensor_scan(endt, ones_e, ntf, 0.0, ALU.mult, ALU.add))
                do(tt(base, endt, ntf, ALU.subtract))
                do(tt(full, full, base, ALU.add))
                do(tsc(base, base, float(P), None, ALU.mult))
                tsc(pad_starts[:, :], full, float(P), None, ALU.mult).then_inc(starts_ready, 1)

            def r_slot_table():
                do(tt(slot_te.rearrange("p t e -> p e t"), work.rearrange("p (e t) -> p e t", t=NT),
                      base.unsqueeze(2).to_broadcast([P, E, NT]), ALU.add))

            def r_weights():
                do(tt(weight_te, scores_te, sel_te, ALU.mult))

            def r_weight_sums():
                do(nc.vector.tensor_reduce(den, weight_te, AX_X, ALU.add))
                do(tsc(den, den, 1e-20, None, ALU.add))
                do(nc.vector.reciprocal(den, den))
                do(tsc(den, den, ROUTE_SCALE, None, ALU.mult))

            def r_weight_table():
                do(tt(weight_te, weight_te, den.unsqueeze(2).to_broadcast([P, NT, E]), ALU.mult))

            def r_tile_experts():
                do(nc.vector.tensor_copy(tile_f[:, :], tile_i[:, :]))
                do(tt(te_cmp, tile_f[:, :].unsqueeze(2).to_broadcast([P, TE_C, E]),
                      endt.unsqueeze(1).to_broadcast([P, TE_C, E]), ALU.is_ge))
                do(nc.vector.tensor_reduce(te_f, te_cmp, AX_X, ALU.add))
                do(tsc(te_f, te_f, float(E - 1), float(WEXP), ALU.min, ALU.mult))
                do(nc.vector.tensor_copy(te_u[:, :], te_f))
                dve.sem_inc(te_ready, 1)
                dve.sem_inc(routing_done, 1)

            def route(g, s):
                if is_(g, 0):
                    if s == 0:
                        r_groups()
                    elif s < CH - 1:
                        r_ranks(s)
                    else:
                        r_ranks(s)
                        r_mask()
                elif is_(g, 1):
                    if s == 1:
                        r_order()
                    elif 2 <= s < 6:
                        r_slots(s - 2)
                    elif s == 6:
                        r_bases()
                    elif s == 7:
                        r_slot_table()

            def route_late(g):
                if is_(g, 0):
                    for s in range(NT // (2 * GT)):
                        r_top8(s)
                    r_select()
                elif is_(g, 1):
                    r_weights()
                    r_weight_sums()
                    r_weight_table()
                    r_tile_experts()

            def a1_norm(n):
                normalise(xn, n, GT).then_inc(xn_ready, 1)

            def bu_scale(n):
                dve.wait_ge(bu_ready, n + 1)
                tt(bu, ps[:, 0, 0:GT * N_STATE].rearrange("p (t n) -> p t n", n=N_STATE),
                   rinv[:, ds(n * GT, GT)].unsqueeze(2).to_broadcast([P, GT, N_STATE]), ALU.mult
                   ).then_inc(bu_scaled, 1)

            def scan(n):
                dve.wait_ge(buT_ready, n + 1)
                nc.vector.tensor_tensor_scan(hs, lam_b, ps[0:N_STATE, 1, :], 0.0, ALU.mult, ALU.add
                                             ).then_inc(hs_ready, 1)

            def make_x1(n, par):
                for t in range(GT):
                    last = nc.vector.scalar_tensor_tensor(z[:, t, :], xn[:, t, :], rinv[:, ds(n * GT + t, 1)],
                                                          skip_w[:, :], ALU.mult, ALU.mult)
                do(last)
                do(tt(z, z, xn, ALU.add))
                dve.wait_ge(y_ready, n + 1)
                for b in range(2):
                    last = tt(x1[:, 2 * b:2 * b + 2, :], z[:, 2 * b:2 * b + 2, :],
                              ps[:, b, :].rearrange("p (t d) -> p t d", d=D), ALU.add)
                last.then_inc(x1_ready, 1)
                dve.wait_ge(x1_ready, n + 1)
                dve.wait_ge(part_stored[par], 8 * (n - par))
                tt(part[par], xs[:, ds(n * GT, GT), :], x1, ALU.add)

            def make_z(n):
                dve.wait_ge(rms_z_ready, n + 1)
                do(nc.vector.reciprocal(rz[:, :], ssz[:, :]))
                for t in range(GT):
                    last = tsc(z[:, t, :], x1[:, t, :], rz[:, t:t + 1], None, ALU.mult)
                last.then_inc(z_ready, 1)

            def h_tile(g, s):
                m = f_rows(s)
                dve.wait_ge(gate_ready, CH * g + s + 1)
                tt(h[0:m, s, :], gate[s % 2][0:m, :], ps[0:m, 3 + 2 * (s % 2), :], ALU.mult).then_inc(h_made, 1)

            def stage_meta_half(i, half):
                ks = slice(K // 2 * half, K // 2 * (half + 1))
                shape = [P, K // 2, E]
                if is_(i, 0):
                    dve.wait_ge(routing_done, 1)
                else:
                    dve.wait_ge(scattered[half], 16 * (K // 2) * i)
                do(tt(eq, order_te[:, ds(i, 1), :].to_broadcast(shape),
                      order_c[:, ks].unsqueeze(2).to_broadcast(shape), ALU.is_equal))
                tt(eq_w, eq, weight_te[:, ds(i, 1), :].to_broadcast(shape), ALU.mult)
                do(tt(eq_s, eq, slot_te[:, ds(i, 1), :].to_broadcast(shape), ALU.mult))
                nc.vector.tensor_reduce(stage[:, ks, D + 1], eq_w, AX_X, ALU.add)
                nc.vector.tensor_copy(stage[:, ks, D].bitcast(U32), codes[:, ds(i, 1)].to_broadcast([P, K // 2]))
                with nc.allow_low_precision(reason="one term of each sum isn't zero, an integer below 2**24"):
                    nc.vector.tensor_reduce(stage_idx[:, ks], eq_s, AX_X, ALU.add
                                            ).then_inc(stage_meta[half], 1)

            def finish_part(g, par):
                dve.wait_ge(down_ready, g + 1)
                for b in range(2):
                    last = tt(part[par][:, 2 * b:2 * b + 2, :], part[par][:, 2 * b:2 * b + 2, :],
                              ps[:, 6 + b, :].rearrange("p (t d) -> p t d", d=D), ALU.add)
                last.then_inc(part_ready, 1)

            def dve_group(g, par):
                more = not is_(g, GROUPS - 1)
                if more:
                    a1_norm(g + 1)
                for s in range(CH):
                    if not is_(g, 0) or s >= 2:
                        h_tile(g, s)
                    route(g, s)
                    for i, half in staged(g, HALVES.get(s, [])):
                        stage_meta_half(i, half)
                    if more and s == 2:
                        bu_scale(g + 1)
                    if more and s == 3:
                        scan(g + 1)
                    if more and s == 4:
                        make_x1(g + 1, 1 - par)
                if more:
                    make_z(g + 1)
                route_late(g)
                for i, half in staged(g, LATE_HALVES):
                    stage_meta_half(i, half)
                finish_part(g, par)

            a1_norm(0)
            do(tt(rinv[:, :], mv[:, :, 1], rstd[:, :], ALU.mult))
            tt(rinv[:, :], rinv[:, :], rstd[:, :], ALU.mult).then_inc(ms_x_ready, 1)
            dve.wait_ge(consts_loaded, 16 * CONSTS)
            for c in range(DC):
                last = tsc(bT[:, c, :], bT[:, c, :], ssmw_col[:, c:c + 1], None, ALU.mult)
            last.then_inc(bT_folded, 1)
            nc.vector.memset(lam_b, 1.0)
            do(tt(skip_w[:, :], skip_w[:, :], ssmw_row[:, :], ALU.mult))
            dve.wait_ge(rms_x_ready, 1)
            do(nc.vector.reciprocal(rinv[:, :], rinv[:, :]))
            bu_scale(0)
            dve.wait_ge(lam_ready, 1)
            do(tsc(lam_b, lam_b, lam[:, :], None, ALU.mult))
            scan(0)
            for c in range(DC):
                for m in range(2):
                    last = tsc(w13[:, m, c, :], w13[:, m, c, :], ffnw_col[:, c:c + 1], None, ALU.mult)
            last.then_inc(w13_folded, 1)
            make_x1(0, 0)
            h_tile(0, 0)
            h_tile(0, 1)
            r_pairs()
            make_z(0)
            groups(dve, dve_group, step, 2 * (4 * BATCH + 3))

            def e_hidden(n, par):
                dve.wait_ge(eg_ready, n + 1)
                tt(eh[par], eg[par], ps[:, 2 + par, :].rearrange("p (s u i) -> p s u i", s=2, u=2)[:, :, 1, :],
                   ALU.mult).then_inc(eh_ready, 1)

            def e_out(n, q):
                dve.wait_ge(ey_ready, n + 1)
                tsc(ey[q][:, 1, :], ps[:, 7, 0:D], rows[q][:, 1, D + 1:D + 2], None, ALU.mult
                    ).then_inc(ey_dve, 1)

            def ehT_copy(n, par):
                dve.wait_ge(ehposed, n + 1)
                nc.vector.tensor_copy(ehT[par], ps[:, 4 + par, 0:2 * P]).then_inc(ehT_ready, 1)

            def dve_pair(n, q):
                e_hidden(n, q % 2)
                e_out(n - 1, (q + RING - 1) % RING)
                ehT_copy(n, q % 2)

            e_hidden(0, 0)
            ehT_copy(0, 0)
            pairs(dve, dve_pair)
            e_out(PAIRS - 1, RING - 1)

            def sum_accs(it):
                for q in range(4):
                    y = f_in[q]
                    dve.wait_ge(f_loaded[q], 16 * ACCS * (it + 1))
                    tt(y[0], y[0], y[1], ALU.add)
                    do(tt(y[2], y[2], y[3], ALU.add))
                    if not is_(it, 0):
                        dve.wait_ge(f_stored[q], 16 * it)
                    tt(f_out[q], y[0], y[2], ALU.add).then_inc(f_summed[q], 1)

            sum_accs(0)
            with dve.Fori(1, FN // 4) as it:
                step.enter(it - 1, 4)
                sum_accs(it)
                step.leave(FN // 4 - 1)

        @block.tensor
        def _(pe):
            mm, tp = nc.tensor.matmul, nc.tensor.transpose

            def a0_transpose(g, par):
                pe.wait_ge(a0_xn_dve, g + 1)
                pe.wait_ge(a0_xn_act, g + 1)
                for c in range(DC):
                    for t in range(GT):
                        last = tp(ps[:, 2 * par + c, t * P:(t + 1) * P], a0_xn[par][:, t, c * P:(c + 1) * P],
                                  ident[:, :])
                last.then_inc(a0_xposed, 1)

            def a0_router(g, par):
                pe.wait_ge(a0_xT_ready, g + 1)
                for c in range(DC):
                    last = mm(ps[0:E, 4 + par, :], gT[:, c, :], a0_xT[par][:, c, :], start=c == 0, stop=c == DC - 1)
                last.then_inc(a0_products_ready, 1)

            def a0_logits(g, par):
                apart(pe, (a0_lT_ready, g + 1))
                for t in range(GT):
                    last = tp(ps[:, 6 + par, t * E:(t + 1) * E], a0_lT[par][:, t * P:(t + 1) * P], ident[0:E, 0:E])
                last.then_inc(a0_logits_ready, 1)

            pe.wait_ge(consts_made, 1)
            pe.wait_ge(router_loaded, 16)

            def pe_a0(g, j):
                if exists(g + 1):
                    a0_transpose(g + 1, (j + 1) % 2)
                if exists(g):
                    a0_router(g, j % 2)
                if exists(g - 1):
                    a0_logits(g - 1, (j + 1) % 2)

            a0_groups(pe, pe_a0)
            a0_logits(GROUPS - 1, 1)

            def rank_product(b):
                if b == 0:
                    pe.wait_ge(sel_et_ready, 1)
                    pe.wait_ge(part_ready, 1)
                else:
                    pe.wait_ge(ranks_used, b)
                mm(ps[:, 6, :], ones_bf[:, :], sel_et[:, 512 * b:512 * (b + 1)], start=True, stop=True)
                mm(ps[:, 7, :], before[:, :], sel_et[:, 512 * b:512 * (b + 1)], start=True, stop=True
                   ).then_inc(ranks_ready, 1)

            def transpose_group(n, src, ready, posed):
                pe.wait_ge(ready, n + 1)
                for c in range(DC):
                    for t in range(GT):
                        last = tp(ps[:, c, t * P:(t + 1) * P], src[:, t, c * P:(c + 1) * P], ident[:, :])
                last.then_inc(posed, 1)

            def bu_product(n):
                pe.wait_ge(xT_ready, n + 1)
                for t in range(GT):
                    for c in range(DC):
                        last = mm(ps[:, 0, t * N_STATE:(t + 1) * N_STATE], xT[:, c, t * P:(t + 1) * P],
                                  bT[:, c, :], start=c == 0, stop=c == DC - 1)
                last.then_inc(bu_ready, 1)

            def bu_transpose(n):
                apart(pe, (bu_scaled, n + 1))
                for t in range(GT):
                    last = tp(ps[0:N_STATE, 1, t * P:(t + 1) * P], bu[:, t, :], ident[:, :])
                last.then_inc(buT_ready, 1)

            def y_product(n):
                pe.wait_ge(hs_ready, n + 1)
                for t in range(GT):
                    last = mm(ps[:, t // 2, (t % 2) * D:(t % 2 + 1) * D], hs[:, t * P:(t + 1) * P], cT[:, :],
                              start=True, stop=True)
                last.then_inc(y_ready, 1)

            def gu_product(g, s):
                if not is_(g, 0) or s >= 2:
                    pe.wait_ge(h_made, CH * g + s - 1)
                m = f_rows(s)
                src = xT if s < 2 else zT
                w = shgu if s < 2 else w13
                lo = P * (s if s < 2 else s - 2)
                for u in range(2):
                    for c in range(DC):
                        last = mm(ps[0:m, 2 + 2 * (s % 2) + u, :], w[:, u, c, lo:lo + m], src[:, c, :],
                                  start=c == 0, stop=c == DC - 1)
                last.then_inc(gu_ready, 1)

            def down_product(g):
                pe.wait_ge(h_made, CH * (g + 1) - 1)
                if not is_(g, 0):
                    pe.wait_ge(part_ready, g)
                for t in range(GT):
                    for s in range(CH):
                        m = f_rows(s)
                        if t == 0 and s == CH - 1:
                            pe.wait_ge(h_made, CH * (g + 1))
                        w = shd[:, s, :] if s < 2 else w2[0:m, s - 2, :]
                        last = mm(ps[:, 6 + t // 2, (t % 2) * D:(t % 2 + 1) * D], h[0:m, s, t * P:(t + 1) * P], w,
                                  start=s == 0, stop=s == CH - 1)
                last.then_inc(down_ready, 1)

            def pe_group(g, par):
                more = not is_(g, GROUPS - 1)
                for s in range(CH):
                    if not is_(g, 0) or s >= 2:
                        gu_product(g, s)
                    if is_(g, 1) and 2 <= s < 6:
                        rank_product(s - 2)
                    if s == 1:
                        pe.wait_ge(zT_ready, g + 1)
                    if more and s == 1:
                        transpose_group(g + 1, xn, xn_ready, xposed)
                    if more and s == 2:
                        bu_product(g + 1)
                    if more and s == 3:
                        bu_transpose(g + 1)
                    if more and s == 4:
                        y_product(g + 1)
                down_product(g)
                if more:
                    transpose_group(g + 1, z, z_ready, zposed)

            transpose_group(0, xn, xn_ready, xposed)
            pe.wait_ge(bT_folded, 1)
            pe.wait_ge(consts_loaded, 16 * CONSTS)
            bu_product(0)
            gu_product(0, 0)
            bu_transpose(0)
            gu_product(0, 1)
            y_product(0)
            pe.wait_ge(w13_folded, 1)
            transpose_group(0, z, z_ready, zposed)
            groups(pe, pe_group)

            def r_transpose(n, q):
                pe.wait_ge(rows_loaded[q], 16 // RING * (n - q) + 16)
                for s in range(2):
                    for c in range(DC):
                        j = 2 * s + c
                        last = tp(ps[:, q % 2, j * P:(j + 1) * P], rows[q][:, s, c * P:(c + 1) * P], ident[:, :])
                last.then_inc(rposed, 1)

            def e_gu(n, par, offsets):
                pe.wait_ge(rT_ready, n + 1)
                for s in range(2):
                    for c in range(DC):
                        j = 2 * s + c
                        last = mm(ps[:, 2 + par, s * D:(s + 1) * D], rT[par][:, j * P:(j + 1) * P],
                                  big[:, ds(offsets[s] + c * D, D)], start=c == 0, stop=c == DC - 1)
                last.then_inc(egu_ready, 1)

            def e_transpose(n, par):
                pe.wait_ge(eh_ready, n + 1)
                for s in range(2):
                    last = tp(ps[:, 4 + par, s * P:(s + 1) * P], eh[par][:, s, :], ident[:, :])
                last.then_inc(ehposed, 1)

            def e_down(n, par, offsets):
                pe.wait_ge(ey_act, n)
                pe.wait_ge(ehT_ready, n + 1)
                for s in range(2):
                    last = mm(ps[:, 6 + s, 0:D], ehT[par][:, s * P:(s + 1) * P],
                              big[:, ds(offsets[s] + 2 * D, D)], start=True, stop=True)
                last.then_inc(ey_ready, 1)

            regs = [[pe.alloc_register(f"offset{j}_{k}") for k in range(4)] for j in range(3)]

            def load_offsets(n, first):
                for j in range(first, 3):
                    pe.load(regs[j], te_row[0:1, ds(2 * n + 4 * (j - first) - 4 * (1 - first), 4)])

            def offsets_of(j):
                return [pe.snap(regs[j // 2][2 * (j % 2) + s], min_val=0, max_val=(E - 1) * WEXP) for s in range(2)]

            def pe_pair(n, q):
                e_gu(n, q % 2, offsets_of(q % 4 + 2))
                if not is_(n, PAIRS - 1):
                    r_transpose(n + 1, (q + 1) % RING)
                e_down(n - 1, (q + 1) % 2, offsets_of(q % 4 + 1))
                if q % 4 == 3 and not is_(n, PAIRS - 1):
                    load_offsets(n + 1, 0)
                e_transpose(n, q % 2)

            pe.wait_ge(te_loaded, 16)
            r_transpose(0, 0)
            pe.wait_ge(wexp_loaded, 16 * (LAST - FIRST + 1))
            load_offsets(0, 1)
            e_gu(0, 0, offsets_of(2))
            r_transpose(1, 1)
            e_transpose(0, 0)
            pairs(pe, pe_pair)
            e_down(PAIRS - 1, 1, offsets_of(5))


def kernel(**inputs):
    import numpy as np
    import concourse.bacc as bacc
    from concourse.bass_utils import run_bass_kernel_spmd

    a = {k.replace("L0_attn_", "").replace("L0_ffn_", "f_"): np.asarray(v) for k, v in inputs.items()}

    def split(m):
        return m.reshape(-1, P, m.shape[1]).transpose(1, 0, 2)

    gu = np.concatenate([a["f_w_gate"], a["f_w_up"]], axis=1).transpose(2, 0, 1)
    gu = gu.reshape(DC, P, E, 2 * INNER).transpose(1, 2, 0, 3).reshape(P, E, DC * 2 * INNER)
    wexp = np.concatenate([gu, a["f_w_down"].transpose(2, 0, 1)], axis=2).reshape(P, E * WEXP)
    arrays = {
        "x": a["x"].reshape(-1, D),
        "log_lambda": a["log_lambda"],
        "BT": split(a["B_w"].T),
        "CT": a["C_w"].T,
        "D_skip": a["D_skip"],
        "ssm_w": a["ssm_norm_w"],
        "ssm_w_col": a["ssm_norm_w"].reshape(DC, P).T,
        "ffn_w_col": a["ffn_norm_w"].reshape(DC, P).T,
        "w13T": np.stack([split(a["w1"].T), split(a["w3"].T)], axis=1),
        "w2T": a["w2"].T,
        "gateT": split(a["f_gate_w"].T),
        "gate_bias": a["f_gate_bias"],
        "wexp": wexp,
        "shguT": np.stack([split(a["f_sh_gate"].T), split(a["f_sh_up"].T)], axis=1),
        "shdT": split(a["f_sh_down"].T),
    }
    nc = bacc.Bacc("TRN2", target_bir_lowering=False, num_devices=1)
    arrays = {f"in_{k}": np.ascontiguousarray(v) for k, v in arrays.items()}
    args = [nc.dram_tensor(k, v.shape, mybir.dt.from_np(v.dtype), kind="ExternalInput").ap()
            for k, v in arrays.items()]
    out = nc.dram_tensor("out", arrays["in_x"].shape, F32, kind="ExternalOutput").ap()
    build(nc, *args, out)
    r = run_bass_kernel_spmd(nc, [arrays], core_ids=[0])
    return r.results[0]["out"].reshape(a["x"].shape)
```

```python
from contextlib import ExitStack

import concourse.bass as bass
from concourse import mybir

P = 128
F32 = mybir.dt.float32
BF16 = mybir.dt.bfloat16
U32 = mybir.dt.uint32
ALU = mybir.AluOpType
ACT = mybir.ActivationFunctionType
AX_X = mybir.AxisListType.X
ds = bass.ds

D = 256
DC = D // P
N_STATE = 64
D_FF = 688
FT = -(-D_FF // P)
E = 32
NG = 8
EG = E // NG
TOP_GROUPS = 4
K = 8
INNER = 128
SHARED = 256
ROUTE_SCALE = 2.5
LN_EPS = 1e-5
RMS_EPS = 1e-6
ACCS = 4
ROW = D + 2
WEXP = 3 * D
GT = 4
G = GT * P


def is_(i, n):
    return isinstance(i, int) and i == n


class Steps:

    def __init__(self, eng, sem):
        self.eng, self.sem, self.base, self.n = eng, sem, 0, 0

    def done(self, ins):
        ins.then_inc(self.sem, 1)
        self.n += 1

    def wait(self):
        self.eng.wait_ge(self.sem, self.base + self.n)

    def enter(self, i, per):
        self.start = (self.base, self.n, per)
        self.base, self.n = self.base + self.n + i * per, 0

    def leave(self, count):
        base, n, per = self.start
        assert self.n == per, (self.n, per)
        self.base, self.n = base + n + count * per, 0


def build(nc, x, log_lambda, BT, CT, D_skip, ssm_w, ssm_w_col, ffn_w_col, w13T, w2T, gateT, gate_bias, wexp,
          shguT, shdT, out):
    T = x.shape[0]
    NT = T // P
    GROUPS = T // G
    NTILE = T * K // P + E
    NSLOT = NTILE * P
    PAIRS = NTILE // 2
    RING = 8
    CH = FT + SHARED // P
    TE_C = -(-NTILE // P)
    W = NT * E
    MAIN = GROUPS - 3
    FIRST = 1
    EARLY = 8
    BATCH = 11
    LAST = FIRST + -(-(2 * NT - EARLY) // BATCH)
    STAGED = 58
    CHUNK = 5
    FW = 2 * D
    UT = P * FW // D
    UNITS = MAIN * G // UT
    LOOP = 4
    assert LAST == MAIN - 1 == 3 + 2 * LOOP + 1 and GROUPS == 16 and PAIRS % RING == 0 and RING == CH
    assert STAGED % 2 == 0 and 2 * STAGED <= EARLY + (LAST - 1 - FIRST) * BATCH and BATCH * LOOP % 4 == 0
    assert all(CHUNK * (g - 1) <= min((EARLY + BATCH * (g - 1)) // 2, GT * (g + 2)) for g in range(FIRST + 1, LAST))

    sorted_rows = nc.dram_tensor("sorted_rows", [NSLOT + P, ROW], F32).ap()
    accs = [nc.dram_tensor(f"acc{a}", [T + P, D], F32).ap() for a in range(ACCS)]
    tile_expert_dram = nc.dram_tensor("tile_expert_dram", [P * TE_C], U32).ap()

    with ExitStack() as ctx:
        def sb(name, shape, dt=F32):
            return ctx.enter_context(nc.sbuf_tensor(name, shape, dt))

        def sem(name):
            return ctx.enter_context(nc.semaphore(name))

        big = sb("big", [P, E * WEXP])
        xs = big[:, 0:NT * D].rearrange("p (t d) -> p t d", d=D)
        tables = big[:, NT * D:NT * D + 3 * W].rearrange("p (k n) -> p k n", k=3)
        order_te = tables[:, 0, :].rearrange("p (t e) -> p t e", e=E)
        weight_te = tables[:, 1, :].rearrange("p (t e) -> p t e", e=E)
        slot_te = tables[:, 2, :].rearrange("p (t e) -> p t e", e=E)

        w13 = sb("w13", [P, 2, DC, D_FF])
        w2 = sb("w2", [P, FT, D])
        shgu = sb("shgu", [P, 2, DC, SHARED])
        shd = sb("shd", [P, SHARED // P, D])
        bT = sb("bT", [P, DC, N_STATE])
        cT = sb("cT", [N_STATE, D])
        gT = sb("gT", [P, DC, E])
        skip_w = sb("skip_w", [P, D])
        ssmw_row = sb("ssmw_row", [P, D])
        ssmw_col = sb("ssmw_col", [P, DC])
        ffnw_col = sb("ffnw_col", [P, DC])
        bias_row = sb("bias_row", [P, E])
        loglam = sb("loglam", [N_STATE, 1])
        lam = sb("lam", [N_STATE, 1])
        ident = sb("ident", [P, P])
        before = sb("before", [P, P], BF16)
        ones_bf = sb("ones_bf", [P, P], BF16)
        codes = sb("codes", [P, NT], U32)
        order_c = sb("order_c", [P, K])
        ln_eps = sb("ln_eps", [P, 1])
        rms_eps = sb("rms_eps", [P, 1])
        stages = [sb(f"stage{j}", [P, K, ROW]) for j in range(2)]
        stage_idx = [sb(f"stage_idx{j}", [P, K], U32) for j in range(2)]
        x_tail = sb("x_tail", [P, GT, D])
        meta = sb("meta", [P, 3, K // 2, E])
        eq, eq_w, eq_s = (meta[:, j, :, :] for j in range(3))
        pad_row = sb("pad_row", [P, ROW])
        pad_starts = sb("pad_starts", [P, E], U32)
        bn6 = sb("bn6", [P, 2, GT, 6])
        mv4 = sb("mv4", [P, 2, GT, 2])
        mv = sb("mv", [P, NT, 2])
        rstd = sb("rstd", [P, NT])
        nmr = sb("nmr", [P, NT])
        rinv = sb("rinv", [P, NT])
        ssz = sb("ssz", [P, GT])
        rz = sb("rz", [P, GT])
        te_u = sb("te_u", [P, TE_C], U32)
        te_row = sb("te_row", [1, P * TE_C], U32)

        ARENA = 13568
        arena = sb("arena", [P, ARENA])
        at = [0]

        def take(n):
            at[0] += n
            assert at[0] <= ARENA
            return arena[:, at[0] - n:at[0]]

        xn = take(GT * D).rearrange("p (t d) -> p t d", d=D)
        xT = take(DC * G).rearrange("p (c n) -> p c n", c=DC)
        bu = take(GT * N_STATE).rearrange("p (t n) -> p t n", n=N_STATE)
        hs = take(G)[0:N_STATE, :]
        lam_b = take(G)[0:N_STATE, :]
        at_x1 = at[0]
        x1 = take(GT * D).rearrange("p (t d) -> p t d", d=D)
        at_z = at[0]
        z = take(GT * D).rearrange("p (t d) -> p t d", d=D)
        at_zT = at[0]
        zT = take(DC * G).rearrange("p (c n) -> p c n", c=DC)
        at_h = at[0]
        h = take(CH * G).rearrange("p (f n) -> p f n", n=G)
        gate = [take(G) for _ in range(2)]
        at_part = at[0]
        part = [take(GT * D).rearrange("p (t d) -> p t d", d=D) for _ in range(2)]
        at[0] = at_h
        a0_xn = [take(GT * D).rearrange("p (t d) -> p t d", d=D) for _ in range(2)]
        a0_xT = [take(DC * G).rearrange("p (c n) -> p c n", c=DC) for _ in range(2)]
        a0_lT = [take(G)[0:E, :] for _ in range(2)]
        assert at[0] <= at_part
        spare = big[:, NT * D + 3 * W:]
        sel_et = spare[:, 0:W // 2].bitcast(BF16)
        restart_te = spare[:, W // 2:W].bitcast(BF16)
        restart_et = sb("restart_et", [P, 512], BF16)
        flat_stages = [st[:, :, :].rearrange("p k w -> p (k w)") for st in stages]
        work, sel = (st[:, 0:W] for st in flat_stages)
        logits, masked = tables[:, 0, :], tables[:, 0, :]
        scores = tables[:, 1, :]
        sc = tables[:, 2, :]
        repl = work
        masked_te, repl_te, sel_te, work_te = (
            a.rearrange("p (t e) -> p t e", e=E) for a in (masked, repl, sel, work))
        scores_te = scores.rearrange("p (t e) -> p t e", e=E)
        hi01, lo01, hi23, lo23 = (work[:, k * NT * NG:(k + 1) * NT * NG] for k in range(4))
        gs, rank, beats = (sel[:, k * NT * NG:(k + 1) * NT * NG] for k in range(3))
        gs_tg, rank_tg, beats_tg = (a.rearrange("p (t g) -> p t g", g=NG) for a in (gs, rank, beats))
        flat_meta = meta[:, :, :, :].rearrange("p a k e -> p (a k e)")
        ne, ntf, endt, base, nt_f, ones_e, full_f = (flat_meta[:, j * E:(j + 1) * E] for j in range(7))
        nt_u, full_u = nt_f.bitcast(U32), full_f.bitcast(U32)
        full = flat_meta[:, 7 * E:8 * E]
        den = flat_meta[:, 8 * E:8 * E + NT]
        te_cmp = sel[:, 0:TE_C * E].rearrange("p (c e) -> p c e", e=E)
        te_f = sel[:, TE_C * E:TE_C * E + TE_C]
        tile_i = sb("tile_i", [P, TE_C], U32)
        tile_f = sb("tile_f", [P, TE_C])
        max8 = sb("max8", [P, 2, GT * 2, K])
        rows = [st[:, 2 * ROW * j:2 * ROW * (j + 1)].rearrange("p (s w) -> p s w", w=ROW)
                for st in flat_stages for j in range(RING // 2)]
        at[0] = 0
        eg = [take(2 * INNER).rearrange("p (s i) -> p s i", i=INNER) for _ in range(2)]
        eh = [take(2 * INNER).rearrange("p (s i) -> p s i", i=INNER) for _ in range(2)]
        assert at[0] <= GT * D
        at[0] = at_z
        rT = [take(2 * D) for _ in range(2)]
        assert at[0] <= at_zT
        at[0] = at_h
        ey = [take(2 * D).rearrange("p (s d) -> p s d", d=D) for _ in range(RING)]
        wgu = [take(4 * INNER * 2).rearrange("p (s w) -> p s w", s=2)]
        assert at[0] <= at_part
        at[0] = at_x1
        wgu.append(take(4 * INNER * 2).rearrange("p (s w) -> p s w", s=2))
        assert at[0] <= at_z
        at_big = [0]

        def take_big(n):
            at_big[0] += n
            return big[:, at_big[0] - n:at_big[0]]

        f_in = [[take_big(FW) for _ in range(ACCS)] for _ in range(4)]
        f_out = [take_big(FW) for _ in range(4)]
        f_tail = [[take_big(GT * D).rearrange("p (t d) -> p t d", d=D) for _ in range(ACCS)]
                  for _ in range(MAIN, GROUPS)]
        x_last = take_big(GT * D).rearrange("p (t d) -> p t d", d=D)
        assert at_big[0] <= E * WEXP

        ps = ctx.enter_context(nc.psum_tensor("ps", [P, 8, 512], F32))

        x_loaded = [sem(f"x_loaded{j}") for j in range(4)]
        router_loaded = sem("router_loaded")
        consts_loaded = sem("consts_loaded")
        consts_made = sem("consts_made")
        pool_step = sem("pool_step")
        dve_step = sem("dve_step")
        act_step = sem("act_step")
        var_ready = sem("var_ready")
        std_ready = sem("std_ready")
        nmr_ready = sem("nmr_ready")
        a0_xn_dve = sem("a0_xn_dve")
        a0_xn_act = sem("a0_xn_act")
        a0_xposed = sem("a0_xposed")
        a0_xT_ready = sem("a0_xT_ready")
        a0_products_ready = sem("a0_products_ready")
        a0_lT_ready = sem("a0_lT_ready")
        a0_logits_ready = sem("a0_logits_ready")
        logits_kept = sem("logits_kept")
        ms_x_ready = sem("ms_x_ready")
        scores_ready = sem("scores_ready")
        rms_x_ready = sem("rms_x_ready")
        bT_folded = sem("bT_folded")
        w13_folded = sem("w13_folded")
        sel_ready = sem("sel_ready")
        sel_et_ready = sem("sel_et_ready")
        starts_ready = sem("starts_ready")
        padded = sem("padded")
        padded_by_pool = sem("padded_by_pool")
        accs_zeroed = sem("accs_zeroed")
        ranks_used = sem("ranks_used")
        ranks_ready = sem("ranks_ready")
        routing_done = sem("routing_done")
        te_ready = sem("te_ready")
        te_stored = sem("te_stored")
        te_loaded = sem("te_loaded")
        lam_ready = sem("lam_ready")

        xn_ready = sem("xn_ready")
        xposed = sem("xposed")
        xT_ready = sem("xT_ready")
        bu_ready = sem("bu_ready")
        bu_scaled = sem("bu_scaled")
        buT_ready = sem("buT_ready")
        hs_ready = sem("hs_ready")
        y_ready = sem("y_ready")
        x1_ready = sem("x1_ready")
        rms_z_ready = sem("rms_z_ready")
        z_ready = sem("z_ready")
        zposed = sem("zposed")
        zT_ready = sem("zT_ready")
        gu_ready = sem("gu_ready")
        gate_ready = sem("gate_ready")
        h_made = sem("h_made")
        down_ready = sem("down_ready")
        part_ready = sem("part_ready")
        part_stored = [sem(f"part_stored{j}") for j in range(2)]
        stage_x = [sem(f"stage_x{j}") for j in range(4)]
        stage_meta = [sem(f"stage_meta{j}") for j in range(4)]
        scattered = [sem(f"scattered{j}") for j in range(4)]
        x_tail_loaded = sem("x_tail_loaded")
        x_last_loaded = sem("x_last_loaded")
        wexp_loaded = sem("wexp_loaded")

        rows_loaded = [sem(f"rows_loaded{j}") for j in range(RING)]
        rposed = sem("rposed")
        rT_ready = sem("rT_ready")
        wgu_ready = sem("wgu_ready")
        egu_ready = sem("egu_ready")
        eg_ready = sem("eg_ready")
        eh_ready = sem("eh_ready")
        ey_ready = sem("ey_ready")
        ey_act = sem("ey_act")
        ey_dve = sem("ey_dve")
        ey_stored = [sem(f"ey_stored{j}") for j in range(RING)]
        f_loaded = [sem(f"f_loaded{j}") for j in range(4)]
        f_summed = [sem(f"f_summed{j}") for j in range(4)]
        f_tail_loaded = [sem(f"f_tail_loaded{g}") for g in range(MAIN, GROUPS)]
        f_stored = [sem(f"f_stored{j}") for j in range(4)]

        block = ctx.enter_context(nc.Block())

        CONSTS = 13
        WEXP_LOADS = (LAST - 2) + 1 + 8

        def f_rows(s):
            return P if s < CH - 1 else D_FF - (FT - 1) * P

        def scattered_half(g, s, at):
            if is_(g, FIRST):
                which = {s: [s - CH // 2] for s in range(CH // 2, CH)} | {CH: range(CH // 2, EARLY)}
            elif isinstance(g, int) and not FIRST < g <= LAST:
                which = {}
            elif is_(g, LAST):
                which = {0: [0], 1: [1], 2: [2, 3], 3: [4], 4: [5], 5: [6, 7], 6: [8], 7: [9, 10]}
            else:
                which = {s: [s] for s in range(CH)} | {CH: range(CH, BATCH)}
            tile, half = at
            return [(tile + (half + i) // 2, (half + i) // 2 % 2, (half + i) % 2) for i in which.get(s, [])
                    if not is_(g, LAST) or half + i < 2 * NT]

        F_STEPS = {MAIN: [2, 3, 5, 6, 7, CH, CH, CH], MAIN + 1: [*range(CH), CH], MAIN + 2: [*range(CH), CH]}
        assert sum(map(len, F_STEPS.values())) == UNITS

        def f_steps(g, s):
            if not isinstance(g, int) or g < MAIN:
                return []
            first = sum(len(F_STEPS[k]) for k in range(MAIN, g))
            return [first + i for i, at_s in enumerate(F_STEPS[g]) if at_s == s]

        def apart(eng, *waits):
            values = [v if isinstance(v, int) else eng.to_reg(v) for _, v in waits]
            eng.wait_ge(consts_made, 1)
            for (s, _), v in zip(waits, values):
                eng.wait_ge(s, v)

        def groups(eng, body, step=None, per=0):
            def at(g):
                return (0, EARLY + (g - FIRST - 1) * BATCH if g > FIRST else 0)

            for g in range(3):
                body(g, g % 2, at(g))
            with eng.Fori(0, 2) as it:
                if step:
                    step.enter(it, per)
                for j in range(LOOP):
                    body(LOOP * it + 3 + j, (3 + j) % 2, (it * (LOOP * BATCH // 2), at(3 + j)[1]))
                if step:
                    step.leave(2)
            for g in range(MAIN - 2, MAIN):
                body(g, g % 2, at(g))

        LEAD = 3

        def exists(g):
            return not isinstance(g, int) or 0 <= g < GROUPS

        def a0_groups(eng, body, step=None, per=0):
            for g in range(-LEAD, 4):
                body(g, g % 4)
            with eng.Fori(1, GROUPS // 4 - 1) as it:
                if step:
                    step.enter(it - 1, per)
                for j in range(4):
                    body(4 * it + j, j)
                if step:
                    step.leave(GROUPS // 4 - 2)
            for g in range(GROUPS - 4, GROUPS):
                body(g, g % 4)

        def x_of(g):
            if is_(g, GROUPS - 2):
                return x_tail[:, :, :]
            return x_last if is_(g, GROUPS - 1) else xs[:, ds(g * GT, GT), :]

        def first_apart(eng, count, body):
            body(0)
            with eng.Fori(1, count) as i:
                body(i)

        def pairs(eng, body):
            for n in range(1, RING):
                body(n, n)
            with eng.Fori(0, PAIRS // RING - 2) as it:
                for q in range(RING):
                    body(RING * it + RING + q, q)
            for q in range(RING):
                body(PAIRS - RING + q, q)

        def rank_bank(b):
            return [6, 2, 4, 6][b]

        def store_padding(eng, half, done):
            eng.wait_ge(starts_ready, 1)
            eng.wait_ge(padded, 16)
            with eng.Fori(0, E // 2) as e:
                start = eng.value_load(pad_starts[0:1, ds(e + half * (E // 2), 1)], min_val=0, max_val=NSLOT)
                eng.dma_start(sorted_rows[ds(start, P), :], pad_row[:, :]).then_inc(done, 16)

        @block.sync
        def _(sp):
            def load_x(it):
                for j in range(4):
                    if not is_(it, 0):
                        sp.wait_ge(x_loaded[j], 16 * it)
                    sp.dma_start(xs[:, ds((4 * it + j) * GT, GT), :],
                                 x[ds((4 * it + j) * G, G), :].rearrange("(t p) d -> p t d", p=P)
                                 ).then_inc(x_loaded[j], 16)

            load_x(0)
            for dst, src in ((bT[:, :, :], BT), (ssmw_col[:, :], ssm_w_col),
                             (skip_w[:, :], D_skip.partition_broadcast(P)),
                             (ssmw_row[:, :], ssm_w.partition_broadcast(P)),
                             (loglam[:, :], log_lambda.rearrange("(n a) -> n a", a=1)),
                             (bias_row[:, :], gate_bias.partition_broadcast(P)),
                             (cT[:, :], CT), (ffnw_col[:, :], ffn_w_col),
                             (shgu[:, :, :, :], shguT), (w13[:, :, :, :], w13T),
                             (w2[:, 0:FT - 1, :], w2T[0:(FT - 1) * P, :].rearrange("(f p) d -> p f d", p=P)),
                             (w2[0:D_FF - (FT - 1) * P, FT - 1, :], w2T[(FT - 1) * P:, :]),
                             (shd[:, :, :], shdT)):
                sp.dma_start(dst, src).then_inc(consts_loaded, 16)
            with sp.Fori(1, GROUPS // 4) as it:
                load_x(it)
            sp.wait_ge(consts_made, 1)
            sp.dma_start(sorted_rows[T * K:NSLOT, :].rearrange("(t p) w -> p t w", p=P),
                         pad_row[:, :].unsqueeze(1).to_broadcast([P, E, ROW])).then_inc(padded, 16)
            for acc in accs:
                sp.dma_start(acc[T:, :], pad_row[:, 0:D]).then_inc(accs_zeroed, 16)

            def zero_acc(a, g):
                sp.dma_start(accs[a][ds(g * G, G), :].rearrange("(t p) d -> p t d", p=P),
                             pad_row[:, 0:D].unsqueeze(1).to_broadcast([P, GT, D])).then_inc(accs_zeroed, 16)

            def zero_accs(g):
                for a in range(1, ACCS):
                    sp.wait_ge(h_made, CH * g + 2 * a)
                    zero_acc(a, g)
                if isinstance(g, int) and g < GROUPS - MAIN:
                    for a in range(ACCS):
                        zero_acc(a, MAIN + g)

            def turn_tile_experts():
                sp.wait_ge(te_ready, 1)
                sp.dma_start(tile_expert_dram.rearrange("(p c) -> p c", c=TE_C), te_u[:, :]).then_inc(te_stored, 16)
                sp.wait_ge(te_stored, 16)
                sp.dma_start(te_row[:, :], tile_expert_dram.rearrange("(a n) -> a n", a=1)).then_inc(te_loaded, 16)
            def load_wexp(lo, hi):
                sp.dma_start(big[:, lo:hi], wexp[:, lo:hi]).then_inc(wexp_loaded, 16)

            def store_part(g, par, _):
                if is_(g, 1):
                    store_padding(sp, 0, padded)
                zero_accs(g)
                if is_(g, LAST):
                    for first, n in ((0, STAGED), (STAGED, NT - STAGED)):
                        sp.wait_ge(stage_x[3], (first + n) // 2)
                        sp.wait_ge(stage_meta[3], (first + n) // 2)
                        load_wexp(max(first, (LAST - 2) * CHUNK) * D, (first + n) * D)
                        for k in range(3):
                            load_wexp(NT * D + k * W + first * E, NT * D + k * W + (first + n) * E)
                sp.wait_ge(part_ready, g + 1)
                sp.dma_start(accs[0][ds(g * G, G), :].rearrange("(t p) d -> p t d", p=P), part[par]
                             ).then_inc(part_stored[par], 16)
                if is_(g, 1):
                    turn_tile_experts()
                if is_(g, 2):
                    load_wexp(NT * D + 3 * W, E * WEXP)
                if not isinstance(g, int) or FIRST < g < LAST:
                    sp.wait_ge(stage_x[3], (CHUNK + 1) // 2 * (g - 1))
                    at = (g - 2) * CHUNK * D
                    sp.dma_start(big[:, ds(at, CHUNK * D)], wexp[:, ds(at, CHUNK * D)]).then_inc(wexp_loaded, 16)

            sp.dma_start(x_tail[:, :, :], x[(GROUPS - 2) * G:(GROUPS - 1) * G, :].rearrange("(t p) d -> p t d", p=P)
                         ).then_inc(x_tail_loaded, 16)
            groups(sp, store_part)
            for j in range(4):
                sp.wait_ge(scattered[j], 16 * (K // 2) * (NT // 2))

            def load_rows(it):
                for q in range(RING):
                    if not is_(it, 0):
                        sp.wait_ge(ey_stored[q], 32 * it)
                    sp.dma_start(rows[q], sorted_rows[ds((RING * it + q) * 2 * P, 2 * P), :]
                                 .rearrange("(s p) w -> p s w", p=P)).then_inc(rows_loaded[q], 16)

            first_apart(sp, PAIRS // RING, load_rows)
            for q in range(RING):
                sp.wait_ge(ey_stored[q], 32 * (PAIRS // RING))

            def load_sums(u):
                for a in range(ACCS):
                    sp.dma_start(f_in[u % 4][a], accs[a][u * UT:(u + 1) * UT, :].rearrange("(p k) d -> p (k d)", p=P)
                                 ).then_inc(f_loaded[u % 4], 16)

            def load_tail_sums(g):
                for a in range(ACCS):
                    sp.dma_start(f_tail[g - MAIN][a], accs[a][g * G:(g + 1) * G, :]
                                 .rearrange("(t p) d -> p t d", p=P)).then_inc(f_tail_loaded[g - MAIN], 16)

            def store_sums(u):
                sp.wait_ge(f_summed[u % 4], u // 4 + 1)
                sp.dma_start(out[u * UT:(u + 1) * UT, :].rearrange("(p k) d -> p (k d)", p=P), f_out[u % 4]
                             ).then_inc(f_stored[u % 4], 16)
                if u + 4 < UNITS:
                    load_sums(u + 4)

            for u in range(4):
                load_sums(u)
            sp.dma_start(x_last, x[(GROUPS - 1) * G:, :].rearrange("(t p) d -> p t d", p=P)
                         ).then_inc(x_last_loaded, 16)
            for g in range(MAIN, GROUPS):
                for s in range(CH + 1):
                    if s == 4:
                        load_tail_sums(g)
                    for u in f_steps(g, s):
                        store_sums(u)
                sp.wait_ge(part_ready, g + 1)
                sp.dma_start(out[g * G:(g + 1) * G, :].rearrange("(t p) d -> p t d", p=P), part[g % 2]
                             ).then_inc(part_stored[g % 2], 16)
            for q in range(4):
                sp.wait_ge(f_stored[q], 16 * len(range(q, UNITS, 4)))
            for par in range(2):
                sp.wait_ge(part_stored[par], 16 * GROUPS // 2)

        @block.gpsimd
        def _(pool):
            step = Steps(pool, pool_step)
            step.done(nc.gpsimd.memset(ident[:, :], 0.0))
            step.done(nc.gpsimd.memset(before[:, :], 1.0))
            nc.gpsimd.memset(ones_bf[:, :], 1.0)
            for k in range(K):
                nc.gpsimd.memset(order_c[:, k:k + 1], float(k - 100))
            nc.gpsimd.memset(ln_eps[:, :], LN_EPS)
            nc.gpsimd.memset(rms_eps[:, :], RMS_EPS)
            step.done(nc.gpsimd.memset(pad_row[:, :], 0.0))
            nc.gpsimd.iota(codes[:, :], pattern=[[P, NT]], base=0, channel_multiplier=1)
            step.done(nc.gpsimd.memset(restart_te, 1.0))
            step.done(nc.gpsimd.memset(restart_et[:, :], 1.0))
            nc.gpsimd.iota(tile_i[:, :], pattern=[[1, TE_C]], base=0, channel_multiplier=TE_C)
            step.wait()
            nc.gpsimd.affine_select(out=ident[:, :], in_=ident[:, :], compare_op=ALU.not_equal, fill=1.0, base=0,
                                    pattern=[[-1, P]], channel_multiplier=1)
            nc.gpsimd.affine_select(out=before[:, :], in_=before[:, :], compare_op=ALU.is_gt, fill=0.0, base=0,
                                    pattern=[[1, P]], channel_multiplier=-1)
            nc.gpsimd.memset(restart_te.rearrange("p (t e) -> p t e", e=E)[:, :, 0:1], 0.0)
            nc.gpsimd.memset(restart_et[:, :].rearrange("p (e t) -> p e t", t=NT)[:, :, 0:1], 0.0)
            nc.gpsimd.iota(pad_row[:, D:D + 1].bitcast(U32), pattern=[[0, 1]], base=T, channel_multiplier=1
                           ).then_inc(consts_made, 1)
            store_padding(pool, 1, padded_by_pool)
            pool.wait_ge(padded_by_pool, 16 * (E // 2))
            pool.wait_ge(padded, 16 * (E // 2 + 1))

            def scatter_tiles(it):
                for j in range(4):
                    par, half = divmod(j, 2)
                    apart(pool, (stage_x[j], it + 1), (stage_meta[j], it + 1))
                    for k in range(K // 2 * half, K // 2 * (half + 1)):
                        pool.indirect_dma_start(
                            out=sorted_rows,
                            out_offset=bass.IndirectOffsetOnAxis(ap=stage_idx[par][:, k:k + 1], axis=0),
                            in_=stages[par][:, k, :], in_offset=None).then_inc(scattered[j], 16)

            first_apart(pool, NT // 2, scatter_tiles)

            pool.wait_ge(accs_zeroed, 16 * (ACCS + (ACCS - 1) * MAIN + ACCS * (GROUPS - MAIN)))
            for par in range(2):
                pool.wait_ge(part_stored[par], 16 * len(range(par, MAIN, 2)))

            def add_results(it):
                for q in range(RING):
                    waits = [(ey_act, RING * it + (q + 1)), (ey_dve, RING * it + (q + 1))]
                    if q >= 2:
                        waits.append((ey_stored[q - 2], 32 * it + 32))
                    elif not is_(it, 0):
                        waits.append((ey_stored[q + RING - 2], 32 * it))
                    apart(pool, *waits)
                    for s in range(2):
                        pool.indirect_dma_start(
                            out=accs[(2 * q + s) % ACCS],
                            out_offset=bass.IndirectOffsetOnAxis(ap=rows[q].bitcast(U32)[:, s, D:D + 1], axis=0),
                            in_=ey[q][:, s, :], in_offset=None, compute_op=ALU.add).then_inc(ey_stored[q], 16)

            first_apart(pool, PAIRS // RING, add_results)

        @block.scalar
        def _(act):
            step = Steps(act, act_step)
            act.dma_start(gT[:, :, :], gateT).then_inc(router_loaded, 16)
            act.wait_ge(consts_made, 1)

            def a0_std(g):
                act.wait_ge(var_ready, g + 1)
                nc.scalar.activation(rstd[:, ds(g * GT, GT)], mv[:, ds(g * GT, GT), 1], ACT.Sqrt, bias=ln_eps[:, :]
                                     ).then_inc(std_ready, 1)

            def a0_normalise(g, par):
                apart(act, (nmr_ready, g + 1))
                for t in range(GT // 2, GT):
                    i = g * GT + t
                    last = nc.scalar.activation(a0_xn[par][:, t, :], xs[:, ds(i, 1), :].rearrange("p t d -> p (t d)"),
                                                ACT.Identity, bias=nmr[:, ds(i, 1)], scale=rstd[:, ds(i, 1)])
                last.then_inc(a0_xn_act, 1)

            def a0_copy(g, par):
                act.wait_ge(a0_xposed, g + 1)
                for c in range(DC):
                    last = nc.scalar.activation(a0_xT[par][:, c, :], ps[:, 2 * par + c, :], ACT.Copy)
                last.then_inc(a0_xT_ready, 1)

            def a0_copy_products(g, par):
                act.wait_ge(a0_products_ready, g + 1)
                nc.scalar.activation(a0_lT[par], ps[0:E, 4 + par, :], ACT.Copy).then_inc(a0_lT_ready, 1)

            def a0_keep_logits(g, par):
                act.wait_ge(a0_logits_ready, g + 1)
                nc.scalar.activation(logits[:, ds(g * GT * E, GT * E)], ps[:, 6 + par, 0:GT * E], ACT.Copy
                                     ).then_inc(logits_kept, 1)

            def act_a0(g, j):
                if exists(g + 2):
                    a0_normalise(g + 2, j % 2)
                if exists(g + 1):
                    a0_copy(g + 1, (j + 1) % 2)
                if exists(g + 3):
                    a0_std(g + 3)
                if exists(g):
                    a0_copy_products(g, j % 2)
                if exists(g - 1):
                    a0_keep_logits(g - 1, (j + 1) % 2)

            a0_groups(act, act_a0)
            act.wait_ge(ms_x_ready, 1)
            nc.scalar.activation(rinv[:, :], rinv[:, :], ACT.Sqrt, bias=rms_eps[:, :]).then_inc(rms_x_ready, 1)
            a0_keep_logits(GROUPS - 1, 1)

            def xT_copy(n):
                act.wait_ge(xposed, n + 1)
                for c in range(DC):
                    last = nc.scalar.activation(xT[:, c, :], ps[:, c, :], ACT.Copy)
                last.then_inc(xT_ready, 1)

            def rms_z(n):
                act.wait_ge(x1_ready, n + 1)
                for t in range(GT):
                    last = nc.scalar.activation(z[:, t, :], x1[:, t, :], ACT.Square, accum_out=ssz[:, t:t + 1])
                step.done(last)
                step.wait()
                nc.scalar.activation(ssz[:, :], ssz[:, :], ACT.Sqrt, bias=rms_eps[:, :], scale=1.0 / D
                                     ).then_inc(rms_z_ready, 1)

            def zT_copy(n):
                act.wait_ge(zposed, n + 1)
                for c in range(DC):
                    last = nc.scalar.activation(zT[:, c, :], ps[:, c, :], ACT.Copy)
                last.then_inc(zT_ready, 1)

            def gate_tile(g, s):
                act.wait_ge(gu_ready, CH * g + s + 1)
                if not is_(g, 0) or s >= 2:
                    act.wait_ge(h_made, CH * g + s - 1)
                m = f_rows(s)
                nc.scalar.activation(gate[s % 2][0:m, :], ps[0:m, 2 + 2 * (s % 2), :], ACT.Silu
                                     ).then_inc(gate_ready, 1)

            def stage_half(i, par, half):
                if isinstance(i, int) and i < 2:
                    act.wait_ge(routing_done, 1)
                else:
                    apart(act, (scattered[2 * par + half], 4 * K * (i - par)))
                nc.scalar.activation(stages[par][:, K // 2 * half:K // 2 * (half + 1), 0:D],
                                     xs[:, ds(i, 1), :].to_broadcast([P, K // 2, D]), ACT.Identity,
                                     bias=nmr[:, ds(i, 1)], scale=rstd[:, ds(i, 1)]
                                     ).then_inc(stage_x[2 * par + half], 1)

            def act_group(g, par, at=None):
                more = not is_(g, GROUPS - 1)
                for s in range(CH):
                    if not is_(g, 0) or s >= 2:
                        gate_tile(g, s)
                    if more and s == CH - 1:
                        rms_z(g + 1)
                    if more and s == 1:
                        xT_copy(g + 1)
                    for tile_half in scattered_half(g, s, at):
                        stage_half(*tile_half)
                if is_(g, 0):
                    act.wait_ge(sel_ready, 1)
                    nc.scalar.activation(sel_et.rearrange("p (e t) -> p t e", t=NT), sel_te, ACT.Copy
                                         ).then_inc(sel_et_ready, 1)
                for tile_half in scattered_half(g, CH, at):
                    stage_half(*tile_half)
                if more:
                    zT_copy(g + 1)

            xT_copy(0)
            act.wait_ge(consts_loaded, 16 * CONSTS)
            nc.scalar.activation(lam[:, :], loglam[:, :], ACT.Sigmoid).then_inc(lam_ready, 1)
            act.wait_ge(logits_kept, GROUPS)
            nc.scalar.activation(scores, logits, ACT.Sigmoid).then_inc(scores_ready, 1)
            gate_tile(0, 0)
            gate_tile(0, 1)
            rms_z(0)
            zT_copy(0)
            groups(act, act_group, step, LOOP)

            def rT_copy(n, par):
                act.wait_ge(rposed, n + 1)
                nc.scalar.activation(rT[par], ps[:, par, :], ACT.Copy).then_inc(rT_ready, 1)

            def e_gate(n, par):
                act.wait_ge(egu_ready, n + 1)
                nc.scalar.activation(
                    eg[par], ps[:, 2 + par, :].rearrange("p (s u i) -> p s u i", s=2, u=2)[:, :, 0, :], ACT.Silu
                ).then_inc(eg_ready, 1)

            def e_out(n, q):
                act.wait_ge(ey_ready, n + 1)
                nc.scalar.activation(ey[q][:, 0, :], ps[:, 6, 0:D], ACT.Copy, scale=rows[q][:, 0, D + 1:D + 2]
                                     ).then_inc(ey_act, 1)

            def act_pair(n, q):
                e_gate(n, q % 2)
                if not is_(n, PAIRS - 1):
                    rT_copy(n + 1, (q + 1) % 2)
                e_out(n - 1, (q + RING - 1) % RING)

            rT_copy(0, 0)
            e_gate(0, 0)
            rT_copy(1, 1)
            pairs(act, act_pair)
            e_out(PAIRS - 1, RING - 1)

            for g in range(MAIN, GROUPS):
                act_group(g, g % 2, (0, 0))

        @block.vector
        def _(dve):
            step = Steps(dve, dve_step)
            tt, tsc = nc.vector.tensor_tensor, nc.vector.tensor_scalar

            def do(ins):
                step.done(ins)
                step.wait()

            def a0_stats(g, j):
                dve.wait_ge(x_loaded[j], 16 * (g // 4 + 1) if isinstance(g, int) else 4 * (g - j) + 16)
                for t in range(GT):
                    last = nc.vector.bn_stats(bn6[:, j % 2, t, :], xs[:, ds(g * GT + t, 1), :]
                                              .rearrange("p t d -> p (t d)"))
                step.done(last)
                apart(dve, (dve_step, step.base + step.n))
                for t in range(GT):
                    last = nc.vector.bn_aggr(mv4[:, j % 2, t, :], bn6[:, j % 2, t, :])
                do(last)
                nc.vector.tensor_copy(mv[:, ds(g * GT, GT), :], mv4[:, j % 2, :, :]).then_inc(var_ready, 1)

            def normalise(dst, src, g, tiles):
                for t in range(tiles):
                    i = g * GT + t
                    last = tsc(dst[:, t, :], src[:, t, :],
                               rstd[:, ds(i, 1)], nmr[:, ds(i, 1)], ALU.mult, ALU.add)
                return last

            def a0_normalise(g, par):
                of_g = ds(g * GT, GT)
                dve.wait_ge(std_ready, g + 1)
                do(nc.vector.reciprocal(rstd[:, of_g], rstd[:, of_g]))
                do(nc.vector.scalar_tensor_tensor(nmr[:, of_g], mv[:, of_g, 0], -1.0, rstd[:, of_g],
                                                  ALU.mult, ALU.mult))
                dve.sem_inc(nmr_ready, 1)
                if not isinstance(g, int) or g >= 2:
                    dve.wait_ge(a0_xposed, g - 1)
                normalise(a0_xn[par], xs[:, of_g, :], g, GT // 2).then_inc(a0_xn_dve, 1)

            def dve_a0(g, j):
                if exists(g + 2):
                    a0_normalise(g + 2, j % 2)
                if exists(g + 3):
                    a0_stats(g + 3, (j + 3) % 4)

            a0_groups(dve, dve_a0, step, 16)

            def r_pairs():
                dve.wait_ge(scores_ready, 1)
                do(tt(sc.rearrange("p (t e) -> p t e", e=E), scores_te,
                      bias_row[:, :].unsqueeze(1).to_broadcast([P, NT, E]), ALU.add))
                v = [sc.rearrange("p (n j) -> p n j", j=EG)[:, :, j] for j in range(EG)]
                tt(hi01, v[0], v[1], ALU.max)
                tt(lo01, v[0], v[1], ALU.min)
                tt(hi23, v[2], v[3], ALU.max)
                do(tt(lo23, v[2], v[3], ALU.min))

            def r_groups():
                tt(gs, hi01, hi23, ALU.max)
                do(tt(lo01, lo01, lo23, ALU.max))
                do(tt(hi01, hi01, hi23, ALU.min))
                do(tt(hi01, hi01, lo01, ALU.max))
                do(tt(gs, gs, hi01, ALU.add))
                for g in range(NG):
                    last = nc.vector.memset(rank_tg[:, :, g:g + 1], float(NG - 1 - g))
                do(last)

            def r_ranks(s):
                do(tt(beats_tg[:, :, 0:NG - s], gs_tg[:, :, 0:NG - s], gs_tg[:, :, s:NG], ALU.is_ge))
                do(tt(rank_tg[:, :, s:NG], rank_tg[:, :, s:NG], beats_tg[:, :, 0:NG - s], ALU.add))
                do(tt(rank_tg[:, :, 0:NG - s], rank_tg[:, :, 0:NG - s], beats_tg[:, :, 0:NG - s], ALU.subtract))

            def r_mask():
                do(tsc(beats, rank, float(TOP_GROUPS), None, ALU.is_lt))
                do(tt(masked.rearrange("p (n j) -> p n j", j=EG), sc.rearrange("p (n j) -> p n j", j=EG),
                      beats.unsqueeze(2).to_broadcast([P, NT * NG, EG]), ALU.mult))

            def r_top8(s):
                for j in range(2 * GT):
                    last = nc.vector.max(max8[:, s % 2, j, :], masked_te[:, 2 * GT * s + j, :])
                do(last)
                for j in range(2 * GT):
                    t = 2 * GT * s + j
                    last = nc.vector.match_replace(repl_te[:, t, :], max8[:, s % 2, j, :], masked_te[:, t, :], -1e30)
                step.done(last)

            def r_select():
                step.wait()
                tt(sel, repl, masked, ALU.not_equal).then_inc(sel_ready, 1)

            def r_order():
                dve.wait_ge(sel_ready, 1)
                do(nc.vector.tensor_tensor_scan(work, restart_te, sel, 0.0, ALU.mult, ALU.add))
                do(nc.vector.scalar_tensor_tensor(order_te, sel_te, -101.0, work_te, ALU.mult, ALU.add))

            def r_slots(b):
                r = slice(512 * b, 512 * (b + 1))
                counts, ranks = ps[:, rank_bank(b), :], ps[:, rank_bank(b) + 1, :]
                dve.wait_ge(ranks_ready, b + 1)
                do(nc.vector.tensor_tensor_scan(work[:, r], restart_et[:, :], counts, 0.0, ALU.mult, ALU.add))
                do(nc.vector.tensor_copy(ne[:, b * 512 // NT:(b + 1) * 512 // NT],
                                         work[:, r].rearrange("p (e t) -> p e t", t=NT)[:, :, NT - 1]))
                do(tt(work[:, r], work[:, r], counts, ALU.subtract))
                tt(work[:, r], work[:, r], ranks, ALU.add).then_inc(ranks_used, 1)

            def r_bases():
                dve.wait_ge(ranks_used, 4)
                tsc(nt_u, ne, float(P - 1), None, ALU.add)
                do(nc.vector.tensor_copy(full_u, ne))
                tsc(nt_u, nt_u, P.bit_length() - 1, None, ALU.logical_shift_right)
                do(tsc(full_u, full_u, P.bit_length() - 1, None, ALU.logical_shift_right))
                nc.vector.memset(ones_e, 1.0)
                nc.vector.tensor_copy(full, full_u)
                do(nc.vector.tensor_copy(ntf, nt_u))
                do(nc.vector.tensor_tensor_scan(endt, ones_e, ntf, 0.0, ALU.mult, ALU.add))
                do(tt(base, endt, ntf, ALU.subtract))
                do(tt(full, full, base, ALU.add))
                do(tsc(base, base, float(P), None, ALU.mult))
                tsc(pad_starts[:, :], full, float(P), None, ALU.mult).then_inc(starts_ready, 1)

            def r_slot_table():
                do(tt(slot_te.rearrange("p t e -> p e t"), work.rearrange("p (e t) -> p e t", t=NT),
                      base.unsqueeze(2).to_broadcast([P, E, NT]), ALU.add))

            def r_weights():
                do(tt(weight_te, scores_te, sel_te, ALU.mult))

            def r_weight_sums():
                do(nc.vector.tensor_reduce(den, weight_te, AX_X, ALU.add))
                do(tsc(den, den, 1e-20, None, ALU.add))
                do(nc.vector.reciprocal(den, den))
                do(tsc(den, den, ROUTE_SCALE, None, ALU.mult))

            def r_weight_table():
                do(tt(weight_te, weight_te, den.unsqueeze(2).to_broadcast([P, NT, E]), ALU.mult))

            def r_tile_experts():
                do(nc.vector.tensor_copy(tile_f[:, :], tile_i[:, :]))
                do(tt(te_cmp, tile_f[:, :].unsqueeze(2).to_broadcast([P, TE_C, E]),
                      endt.unsqueeze(1).to_broadcast([P, TE_C, E]), ALU.is_ge))
                do(nc.vector.tensor_reduce(te_f, te_cmp, AX_X, ALU.add))
                do(tsc(te_f, te_f, float(E - 1), float(WEXP), ALU.min, ALU.mult))
                do(nc.vector.tensor_copy(te_u[:, :], te_f))
                dve.sem_inc(te_ready, 1)

            def route(g, s):
                if is_(g, 0):
                    if s == 0:
                        r_pairs()
                    elif s == 1:
                        r_groups()
                    elif s < 4:
                        r_ranks(2 * s - 3)
                        r_ranks(2 * s - 2)
                    elif s == 4:
                        r_ranks(5)
                    elif s == 5:
                        r_ranks(6)
                        r_ranks(7)
                        r_mask()
                    else:
                        r_top8(2 * s - 12)
                        r_top8(2 * s - 11)
                elif is_(g, 1):
                    if s == 0:
                        r_slot_table()
                    elif s == 1:
                        r_weights()
                    elif s == 2:
                        r_weight_sums()
                        r_weight_table()
                    elif s == 3:
                        r_tile_experts()
                        dve.sem_inc(routing_done, 1)

            def route_first():
                for b in range(4):
                    r_slots(b)
                r_bases()

            def route_late(g):
                if is_(g, 0):
                    for s in range(4, NT // (2 * GT)):
                        r_top8(s)
                    r_select()
                    r_order()

            def a1_norm(n):
                normalise(xn, x_of(n), n, GT).then_inc(xn_ready, 1)

            def bu_scale(n):
                dve.wait_ge(bu_ready, n + 1)
                tt(bu, ps[:, 0, 0:GT * N_STATE].rearrange("p (t n) -> p t n", n=N_STATE),
                   rinv[:, ds(n * GT, GT)].unsqueeze(2).to_broadcast([P, GT, N_STATE]), ALU.mult
                   ).then_inc(bu_scaled, 1)

            def scan(n):
                dve.wait_ge(buT_ready, n + 1)
                nc.vector.tensor_tensor_scan(hs, lam_b, ps[0:N_STATE, 1, :], 0.0, ALU.mult, ALU.add
                                             ).then_inc(hs_ready, 1)

            def make_x1(n, par):
                for t in range(GT):
                    last = nc.vector.scalar_tensor_tensor(z[:, t, :], xn[:, t, :], rinv[:, ds(n * GT + t, 1)],
                                                          skip_w[:, :], ALU.mult, ALU.mult)
                do(last)
                do(tt(z, z, xn, ALU.add))
                dve.wait_ge(y_ready, n + 1)
                for b in range(2):
                    last = tt(x1[:, 2 * b:2 * b + 2, :], z[:, 2 * b:2 * b + 2, :],
                              ps[:, b, :].rearrange("p (t d) -> p t d", d=D), ALU.add)
                last.then_inc(x1_ready, 1)
                dve.wait_ge(x1_ready, n + 1)
                dve.wait_ge(part_stored[par], 8 * (n - par))
                tt(part[par], x_of(n), x1, ALU.add)

            def make_z(n):
                dve.wait_ge(rms_z_ready, n + 1)
                do(nc.vector.reciprocal(rz[:, :], ssz[:, :]))
                for t in range(GT):
                    last = tsc(z[:, t, :], x1[:, t, :], rz[:, t:t + 1], None, ALU.mult)
                last.then_inc(z_ready, 1)

            def h_tile(g, s):
                m = f_rows(s)
                dve.wait_ge(gate_ready, CH * g + s + 1)
                tt(h[0:m, s, :], gate[s % 2][0:m, :], ps[0:m, 3 + 2 * (s % 2), :], ALU.mult).then_inc(h_made, 1)

            def stage_meta_half(i, par, half):
                ks = slice(K // 2 * half, K // 2 * (half + 1))
                shape = [P, K // 2, E]
                stage = stages[par]
                if isinstance(i, int) and i < 2:
                    dve.wait_ge(routing_done, 1)
                else:
                    dve.wait_ge(scattered[2 * par + half], 4 * K * (i - par))
                do(tt(eq, order_te[:, ds(i, 1), :].to_broadcast(shape),
                      order_c[:, ks].unsqueeze(2).to_broadcast(shape), ALU.is_equal))
                tt(eq_w, eq, weight_te[:, ds(i, 1), :].to_broadcast(shape), ALU.mult)
                do(tt(eq_s, eq, slot_te[:, ds(i, 1), :].to_broadcast(shape), ALU.mult))
                nc.vector.tensor_reduce(stage[:, ks, D + 1], eq_w, AX_X, ALU.add)
                nc.vector.tensor_copy(stage[:, ks, D].bitcast(U32), codes[:, ds(i, 1)].to_broadcast([P, K // 2]))
                with nc.allow_low_precision(reason="one term of each sum isn't zero, an integer below 2**24"):
                    nc.vector.tensor_reduce(stage_idx[par][:, ks], eq_s, AX_X, ALU.add
                                            ).then_inc(stage_meta[2 * par + half], 1)

            def finish_part(g, par):
                dve.wait_ge(down_ready, g + 1)
                for b in range(2):
                    last = tt(part[par][:, 2 * b:2 * b + 2, :], part[par][:, 2 * b:2 * b + 2, :],
                              ps[:, 6 + b, :].rearrange("p (t d) -> p t d", d=D), ALU.add)
                last.then_inc(part_ready, 1)

            def sum_accs(u):
                y = f_in[u % 4]
                dve.wait_ge(f_loaded[u % 4], 16 * ACCS * (u // 4 + 1))
                tt(y[0], y[0], y[1], ALU.add)
                do(tt(y[2], y[2], y[3], ALU.add))
                if u >= 4:
                    dve.wait_ge(f_stored[u % 4], 16 * (u // 4))
                tt(f_out[u % 4], y[0], y[2], ALU.add).then_inc(f_summed[u % 4], 1)

            def sum_tail_accs(g):
                y = f_tail[g - MAIN]
                dve.wait_ge(f_tail_loaded[g - MAIN], 16 * ACCS)
                tt(y[0], y[0], y[1], ALU.add)
                do(tt(y[2], y[2], y[3], ALU.add))
                do(tt(y[0], y[0], y[2], ALU.add))
                do(tt(part[g % 2], part[g % 2], y[0], ALU.add))

            def dve_group(g, par, at=None):
                more = not is_(g, GROUPS - 1)
                if is_(g, MAIN):
                    dve.wait_ge(x_tail_loaded, 16)
                if is_(g, MAIN + 1):
                    dve.wait_ge(x_last_loaded, 16)
                if more:
                    a1_norm(g + 1)
                for s in range(CH):
                    if is_(g, MAIN):
                        dve.wait_ge(ey_stored[s], 32 * (PAIRS // RING))

                    if is_(g, 1) and s == 0:
                        route_first()
                    if not is_(g, 0) or s >= 2:
                        h_tile(g, s)
                    route(g, s)
                    for tile_half in scattered_half(g, s, at):
                        stage_meta_half(*tile_half)
                    for u in f_steps(g, s):
                        sum_accs(u)
                    if more and s == 2:
                        bu_scale(g + 1)
                    if more and s == 3:
                        scan(g + 1)
                    if more and s == 4:
                        make_x1(g + 1, 1 - par)
                if more:
                    make_z(g + 1)
                route_late(g)
                for tile_half in scattered_half(g, CH, at):
                    stage_meta_half(*tile_half)
                for u in f_steps(g, CH):
                    sum_accs(u)
                if isinstance(g, int) and g >= MAIN:
                    sum_tail_accs(g)
                finish_part(g, par)

            a1_norm(0)
            do(tt(rinv[:, :], mv[:, :, 1], rstd[:, :], ALU.mult))
            tt(rinv[:, :], rinv[:, :], rstd[:, :], ALU.mult).then_inc(ms_x_ready, 1)
            dve.wait_ge(consts_loaded, 16 * CONSTS)
            for c in range(DC):
                last = tsc(bT[:, c, :], bT[:, c, :], ssmw_col[:, c:c + 1], None, ALU.mult)
            last.then_inc(bT_folded, 1)
            nc.vector.memset(lam_b, 1.0)
            do(tt(skip_w[:, :], skip_w[:, :], ssmw_row[:, :], ALU.mult))
            dve.wait_ge(rms_x_ready, 1)
            do(nc.vector.reciprocal(rinv[:, :], rinv[:, :]))
            bu_scale(0)
            dve.wait_ge(lam_ready, 1)
            do(tsc(lam_b, lam_b, lam[:, :], None, ALU.mult))
            scan(0)
            for c in range(DC):
                for m in range(2):
                    last = tsc(w13[:, m, c, :], w13[:, m, c, :], ffnw_col[:, c:c + 1], None, ALU.mult)
            last.then_inc(w13_folded, 1)
            make_x1(0, 0)
            h_tile(0, 0)
            h_tile(0, 1)
            make_z(0)
            groups(dve, dve_group, step, LOOP * (2 * BATCH + 3))

            def e_hidden(n, par):
                dve.wait_ge(eg_ready, n + 1)
                tt(eh[par], eg[par], ps[:, 2 + par, :].rearrange("p (s u i) -> p s u i", s=2, u=2)[:, :, 1, :],
                   ALU.mult).then_inc(eh_ready, 1)

            def e_out(n, q):
                dve.wait_ge(ey_ready, n + 1)
                tsc(ey[q][:, 1, :], ps[:, 7, 0:D], rows[q][:, 1, D + 1:D + 2], None, ALU.mult
                    ).then_inc(ey_dve, 1)

            offsets = [dve.alloc_register(f"dve_offset{k}") for k in range(4)]

            def copy_weights(n, q):
                if q % 2 == 0:
                    dve.load(offsets, te_row[0:1, ds(2 * n, 4)])
                for s in range(2):
                    at = dve.snap(offsets[2 * (q % 2) + s], min_val=0, max_val=(E - 1) * WEXP)
                    last = nc.vector.tensor_copy(wgu[q % 2][:, s, :], big[:, ds(at, 4 * INNER)])
                last.then_inc(wgu_ready, 1)

            def dve_pair(n, q):
                if not is_(n, PAIRS - 1):
                    copy_weights(n + 1, (q + 1) % RING)
                e_hidden(n, q % 2)
                e_out(n - 1, (q + RING - 1) % RING)

            dve.wait_ge(te_loaded, 16)
            dve.wait_ge(wexp_loaded, 16 * WEXP_LOADS)
            dve.wait_ge(h_made, CH * MAIN)
            dve.wait_ge(z_ready, MAIN + 1)
            copy_weights(0, 0)
            copy_weights(1, 1)
            e_hidden(0, 0)
            pairs(dve, dve_pair)
            e_out(PAIRS - 1, RING - 1)

            for g in range(MAIN, GROUPS):
                dve_group(g, g % 2, (0, 0))

        @block.tensor
        def _(pe):
            mm, tp = nc.tensor.matmul, nc.tensor.transpose

            def a0_transpose(g, par):
                pe.wait_ge(a0_xn_dve, g + 1)
                pe.wait_ge(a0_xn_act, g + 1)
                for c in range(DC):
                    for t in range(GT):
                        last = tp(ps[:, 2 * par + c, t * P:(t + 1) * P], a0_xn[par][:, t, c * P:(c + 1) * P],
                                  ident[:, :])
                last.then_inc(a0_xposed, 1)

            def a0_router(g, par):
                pe.wait_ge(a0_xT_ready, g + 1)
                for c in range(DC):
                    last = mm(ps[0:E, 4 + par, :], gT[:, c, :], a0_xT[par][:, c, :], start=c == 0, stop=c == DC - 1)
                last.then_inc(a0_products_ready, 1)

            def a0_logits(g, par):
                apart(pe, (a0_lT_ready, g + 1))
                for t in range(GT):
                    last = tp(ps[:, 6 + par, t * E:(t + 1) * E], a0_lT[par][:, t * P:(t + 1) * P], ident[0:E, 0:E])
                last.then_inc(a0_logits_ready, 1)

            pe.wait_ge(consts_made, 1)
            pe.wait_ge(router_loaded, 16)

            def pe_a0(g, j):
                if exists(g + 1):
                    a0_transpose(g + 1, (j + 1) % 2)
                if exists(g):
                    a0_router(g, j % 2)
                if exists(g - 1):
                    a0_logits(g - 1, (j + 1) % 2)

            a0_groups(pe, pe_a0)
            a0_logits(GROUPS - 1, 1)

            def rank_product(b):
                if b == 0:
                    pe.wait_ge(sel_et_ready, 1)
                    pe.wait_ge(part_ready, 1)
                elif b == 3:
                    pe.wait_ge(ranks_used, 1)
                bank = rank_bank(b)
                mm(ps[:, bank, :], ones_bf[:, :], sel_et[:, 512 * b:512 * (b + 1)], start=True, stop=True)
                mm(ps[:, bank + 1, :], before[:, :], sel_et[:, 512 * b:512 * (b + 1)], start=True, stop=True
                   ).then_inc(ranks_ready, 1)

            def transpose_group(n, src, ready, posed):
                pe.wait_ge(ready, n + 1)
                for c in range(DC):
                    for t in range(GT):
                        last = tp(ps[:, c, t * P:(t + 1) * P], src[:, t, c * P:(c + 1) * P], ident[:, :])
                last.then_inc(posed, 1)

            def bu_product(n):
                pe.wait_ge(xT_ready, n + 1)
                for t in range(GT):
                    for c in range(DC):
                        last = mm(ps[:, 0, t * N_STATE:(t + 1) * N_STATE], xT[:, c, t * P:(t + 1) * P],
                                  bT[:, c, :], start=c == 0, stop=c == DC - 1)
                last.then_inc(bu_ready, 1)

            def bu_transpose(n):
                apart(pe, (bu_scaled, n + 1))
                for t in range(GT):
                    last = tp(ps[0:N_STATE, 1, t * P:(t + 1) * P], bu[:, t, :], ident[:, :])
                last.then_inc(buT_ready, 1)

            def y_product(n):
                pe.wait_ge(hs_ready, n + 1)
                for t in range(GT):
                    last = mm(ps[:, t // 2, (t % 2) * D:(t % 2 + 1) * D], hs[:, t * P:(t + 1) * P], cT[:, :],
                              start=True, stop=True)
                last.then_inc(y_ready, 1)

            def gu_product(g, s):
                if not is_(g, 0) or s >= 2:
                    pe.wait_ge(h_made, CH * g + s - 1)
                m = f_rows(s)
                src = xT if s < 2 else zT
                w = shgu if s < 2 else w13
                lo = P * (s if s < 2 else s - 2)
                for u in range(2):
                    for c in range(DC):
                        last = mm(ps[0:m, 2 + 2 * (s % 2) + u, :], w[:, u, c, lo:lo + m], src[:, c, :],
                                  start=c == 0, stop=c == DC - 1)
                last.then_inc(gu_ready, 1)

            def down_product(g):
                pe.wait_ge(h_made, CH * (g + 1) - 1)
                if not is_(g, 0):
                    pe.wait_ge(part_ready, g)
                for t in range(GT):
                    for s in range(CH):
                        m = f_rows(s)
                        if t == 0 and s == CH - 1:
                            pe.wait_ge(h_made, CH * (g + 1))
                        w = shd[:, s, :] if s < 2 else w2[0:m, s - 2, :]
                        last = mm(ps[:, 6 + t // 2, (t % 2) * D:(t % 2 + 1) * D], h[0:m, s, t * P:(t + 1) * P], w,
                                  start=s == 0, stop=s == CH - 1)
                last.then_inc(down_ready, 1)

            def pe_group(g, par, _=None):
                more = not is_(g, GROUPS - 1)
                for s in range(CH):
                    if is_(g, 1) and s == 0:
                        for b in range(4):
                            rank_product(b)
                    if is_(g, 1) and s < 2:
                        pe.wait_ge(ranks_used, 2 + s)
                    if not is_(g, 0) or s >= 2:
                        gu_product(g, s)
                    if s == 1:
                        pe.wait_ge(zT_ready, g + 1)
                    if more and s == 1:
                        transpose_group(g + 1, xn, xn_ready, xposed)
                    if more and s == 2:
                        bu_product(g + 1)
                    if more and s == 3:
                        bu_transpose(g + 1)
                    if more and s == 4:
                        y_product(g + 1)
                down_product(g)
                if more:
                    transpose_group(g + 1, z, z_ready, zposed)

            transpose_group(0, xn, xn_ready, xposed)
            pe.wait_ge(bT_folded, 1)
            pe.wait_ge(consts_loaded, 16 * CONSTS)
            bu_product(0)
            gu_product(0, 0)
            bu_transpose(0)
            y_product(0)
            gu_product(0, 1)
            pe.wait_ge(w13_folded, 1)
            transpose_group(0, z, z_ready, zposed)
            groups(pe, pe_group)

            def r_transpose(n, q):
                pe.wait_ge(rows_loaded[q], 16 // RING * (n - q) + 16)
                for s in range(2):
                    for c in range(DC):
                        j = 2 * s + c
                        last = tp(ps[:, q % 2, j * P:(j + 1) * P], rows[q][:, s, c * P:(c + 1) * P], ident[:, :])
                last.then_inc(rposed, 1)

            def e_gu(n, par):
                pe.wait_ge(rT_ready, n + 1)
                pe.wait_ge(wgu_ready, n + 1)
                for s in range(2):
                    for u in range(2):
                        for c in range(DC):
                            at = (2 * c + u) * INNER
                            last = mm(ps[:, 2 + par, (2 * s + u) * P:(2 * s + u + 1) * P],
                                      wgu[par][:, s, at:at + INNER], rT[par][:, (2 * s + c) * P:(2 * s + c + 1) * P],
                                      start=c == 0, stop=c == DC - 1)
                last.then_inc(egu_ready, 1)

            def e_down(n, par, offsets):
                pe.wait_ge(ey_act, n)
                pe.wait_ge(ey_dve, n)
                pe.wait_ge(eh_ready, n + 1)
                for s in range(2):
                    last = mm(ps[:, 6 + s, 0:D], eh[par][:, s, :], big[:, ds(offsets[s] + 2 * D, D)],
                              start=True, stop=True)
                last.then_inc(ey_ready, 1)

            regs = [[pe.alloc_register(f"offset{j}_{k}") for k in range(4)] for j in range(3)]

            def load_offsets(n, first):
                for j in range(first, 3):
                    pe.load(regs[j], te_row[0:1, ds(2 * n + 4 * (j - first) - 4 * (1 - first), 4)])

            def offsets_of(j):
                return [pe.snap(regs[j // 2][2 * (j % 2) + s], min_val=0, max_val=(E - 1) * WEXP) for s in range(2)]

            def pe_pair(n, q):
                e_gu(n, q % 2)
                if not is_(n, PAIRS - 1):
                    r_transpose(n + 1, (q + 1) % RING)
                e_down(n - 1, (q + 1) % 2, offsets_of(q % 4 + 1))
                if q % 4 == 3 and not is_(n, PAIRS - 1):
                    load_offsets(n + 1, 0)

            pe.wait_ge(te_loaded, 16)
            pe.wait_ge(zT_ready, MAIN + 1)
            r_transpose(0, 0)
            pe.wait_ge(wexp_loaded, 16 * WEXP_LOADS)
            load_offsets(0, 1)
            e_gu(0, 0)
            r_transpose(1, 1)
            pairs(pe, pe_pair)
            e_down(PAIRS - 1, 1, offsets_of(5))

            for g in range(MAIN, GROUPS):
                pe_group(g, g % 2)


def kernel(**inputs):
    import numpy as np
    import concourse.bacc as bacc
    from concourse.bass_utils import run_bass_kernel_spmd

    a = {k.replace("L0_attn_", "").replace("L0_ffn_", "f_"): np.asarray(v) for k, v in inputs.items()}

    def split(m):
        return m.reshape(-1, P, m.shape[1]).transpose(1, 0, 2)

    gu = np.concatenate([a["f_w_gate"], a["f_w_up"]], axis=1).transpose(2, 0, 1)
    gu = gu.reshape(DC, P, E, 2 * INNER).transpose(1, 2, 0, 3).reshape(P, E, DC * 2 * INNER)
    wexp = np.concatenate([gu, a["f_w_down"].transpose(2, 0, 1)], axis=2).reshape(P, E * WEXP)
    arrays = {
        "x": a["x"].reshape(-1, D),
        "log_lambda": a["log_lambda"],
        "BT": split(a["B_w"].T),
        "CT": a["C_w"].T,
        "D_skip": a["D_skip"],
        "ssm_w": a["ssm_norm_w"],
        "ssm_w_col": a["ssm_norm_w"].reshape(DC, P).T,
        "ffn_w_col": a["ffn_norm_w"].reshape(DC, P).T,
        "w13T": np.stack([split(a["w1"].T), split(a["w3"].T)], axis=1),
        "w2T": a["w2"].T,
        "gateT": split(a["f_gate_w"].T),
        "gate_bias": a["f_gate_bias"],
        "wexp": wexp,
        "shguT": np.stack([split(a["f_sh_gate"].T), split(a["f_sh_up"].T)], axis=1),
        "shdT": split(a["f_sh_down"].T),
    }
    nc = bacc.Bacc("TRN2", target_bir_lowering=False, num_devices=1)
    arrays = {f"in_{k}": np.ascontiguousarray(v) for k, v in arrays.items()}
    args = [nc.dram_tensor(k, v.shape, mybir.dt.from_np(v.dtype), kind="ExternalInput").ap()
            for k, v in arrays.items()]
    out = nc.dram_tensor("out", arrays["in_x"].shape, F32, kind="ExternalOutput").ap()
    build(nc, *args, out)
    r = run_bass_kernel_spmd(nc, [arrays], core_ids=[0])
    return r.results[0]["out"].reshape(a["x"].shape)
```
